# Optimizing a Trainium2 kernel written in Bass

```python
import numpy as np
import jax
import jax.numpy as jnp

def _softmax(x, axis=-1):
    return jax.nn.softmax(x, axis=axis)

def _gelu(x):
    return jax.nn.gelu(x, approximate=True)

def _silu(x):
    return jax.nn.silu(x)

def _sigmoid(x):
    return jax.nn.sigmoid(x)

def _layernorm(x, axis=-1, eps=1e-05):
    m = jnp.mean(x, axis=axis, keepdims=True)
    v = jnp.var(x, axis=axis, keepdims=True)
    return (x - m) / jnp.sqrt(v + eps)

def _scatter_add(tgt, idx, src, axis=0):
    return tgt.at[idx].add(src)

def _segment_sum(src, seg, n):
    return jax.ops.segment_sum(src, seg, n)
kernel_name = 'mk_seq_postln_d1_jaxref_r8_c1433a'

def setup_inputs(seed: int=0):
    np.random.seed(seed)
    _w = jnp.asarray

    def _L0_attn_setup():
        import jax, jax.numpy as jnp
        import numpy as np
        B, S, D_IN = (2, 256, 128)
        H, D_HID = (16, 128)
        HD = D_HID // H
        key = jax.random.key(seed)
        ks = jax.random.split(key, 9)
        s_in = 1.0 / np.sqrt(D_IN)
        s_hid = 1.0 / np.sqrt(D_HID * H)
        return {'x': jax.random.normal(ks[0], (B, S, D_IN), dtype=jnp.float32), 'Wq': jax.random.uniform(ks[1], (D_IN, D_HID), jnp.float32, -s_in, s_in), 'bq': jax.random.uniform(ks[2], (D_HID,), jnp.float32, -s_in, s_in), 'Wk': jax.random.uniform(ks[3], (D_IN, D_HID), jnp.float32, -s_in, s_in), 'bk': jax.random.uniform(ks[4], (D_HID,), jnp.float32, -s_in, s_in), 'Wv': jax.random.uniform(ks[5], (D_IN, D_HID), jnp.float32, -s_in, s_in), 'bv': jax.random.uniform(ks[6], (D_HID,), jnp.float32, -s_in, s_in), 'Wo': jax.random.uniform(ks[7], (D_HID, D_HID), jnp.float32, -s_hid, s_hid), 'bo': jax.random.uniform(ks[8], (D_HID,), jnp.float32, -s_hid, s_hid)}
    _L0_attn_in = _L0_attn_setup()

    def _L0_ffn_setup():
        import jax, jax.numpy as jnp
        import numpy as np
        D_MODEL = 128
        H_SHARED = 256
        H_ROUTED = 128
        N_EXPERTS = 8
        TOP_K = 2
        key = jax.random.key(seed)
        ks = jax.random.split(key, 8)
        B, T = (2, 256)
        sc_d = 1.0 / np.sqrt(D_MODEL)
        sc_hs = 1.0 / np.sqrt(H_SHARED)
        sc_hr = 1.0 / np.sqrt(H_ROUTED)
        return {'x': jax.random.normal(ks[0], (B, T, D_MODEL), dtype=jnp.float32), 'router_w': jax.random.normal(ks[1], (N_EXPERTS, D_MODEL), dtype=jnp.float32) * sc_d, 'router_bias': jnp.zeros((N_EXPERTS,), dtype=jnp.float32), 'sw1': jax.random.normal(ks[2], (D_MODEL, H_SHARED), dtype=jnp.float32) * sc_d, 'sw3': jax.random.normal(ks[3], (D_MODEL, H_SHARED), dtype=jnp.float32) * sc_d, 'sw2': jax.random.normal(ks[4], (H_SHARED, D_MODEL), dtype=jnp.float32) * sc_hs, 'ew1': jax.random.normal(ks[5], (N_EXPERTS, D_MODEL, H_ROUTED), dtype=jnp.float32) * sc_d, 'ew2': jax.random.normal(ks[6], (N_EXPERTS, H_ROUTED, D_MODEL), dtype=jnp.float32) * sc_hr}
    _L0_ffn_in = _L0_ffn_setup()
    _d = {'L0_attn_x': _L0_attn_in['x'], 'L0_attn_Wq': _L0_attn_in['Wq'], 'L0_attn_bq': _L0_attn_in['bq'], 'L0_attn_Wk': _L0_attn_in['Wk'], 'L0_attn_bk': _L0_attn_in['bk'], 'L0_attn_Wv': _L0_attn_in['Wv'], 'L0_attn_bv': _L0_attn_in['bv'], 'L0_attn_Wo': _L0_attn_in['Wo'], 'L0_attn_bo': _L0_attn_in['bo'], 'L0_ffn_router_w': _L0_ffn_in['router_w'], 'L0_ffn_router_bias': _L0_ffn_in['router_bias'], 'L0_ffn_sw1': _L0_ffn_in['sw1'], 'L0_ffn_sw3': _L0_ffn_in['sw3'], 'L0_ffn_sw2': _L0_ffn_in['sw2'], 'L0_ffn_ew1': _L0_ffn_in['ew1'], 'L0_ffn_ew2': _L0_ffn_in['ew2']}
    _x0 = _d['L0_attn_x']
    _d['L0_attn_x'] = jax.random.normal(jax.random.fold_in(jax.random.key(seed), 1), (8, 256, 128), dtype=_x0.dtype)
    del _x0
    return _d

def reference(L0_attn_x, L0_attn_Wq, L0_attn_bq, L0_attn_Wk, L0_attn_bk, L0_attn_Wv, L0_attn_bv, L0_attn_Wo, L0_attn_bo, L0_ffn_router_w, L0_ffn_router_bias, L0_ffn_sw1, L0_ffn_sw3, L0_ffn_sw2, L0_ffn_ew1, L0_ffn_ew2):

    def _L0_attn_ref(x, Wq, bq, Wk, bk, Wv, bv, Wo, bo):
        import jax, jax.numpy as jnp
        import numpy as np
        B, S, D_IN = (2, 256, 128)
        H, D_HID = (16, 128)
        HD = D_HID // H
        b, s, _ = x.shape

        def proj(W, bias):
            return (x @ W + bias).reshape(b, s, H, HD).transpose(0, 2, 1, 3)
        Q, K, V = (proj(Wq, bq), proj(Wk, bk), proj(Wv, bv))
        scale = 1.0 / np.sqrt(HD).astype(np.float32)
        scores = jnp.einsum('bhqd,bhkd->bhqk', Q, K) * scale
        attn = jax.nn.softmax(scores, axis=-1)
        attended = jnp.einsum('bhqk,bhkd->bhqd', attn, V)
        attended = attended.transpose(0, 2, 1, 3).reshape(b, s, D_HID)
        return attended @ Wo + bo

    def _L0_ffn_ref(x, router_w, router_bias, sw1, sw3, sw2, ew1, ew2):
        import jax, jax.numpy as jnp
        import numpy as np
        D_MODEL = 128
        H_SHARED = 256
        H_ROUTED = 128
        N_EXPERTS = 8
        TOP_K = 2
        B, T, C = x.shape
        xf = x.reshape(-1, C)
        shared_out = jax.nn.silu(xf @ sw1) * (xf @ sw3) @ sw2
        s = jax.nn.sigmoid((xf @ router_w.T).astype(jnp.float32))
        sel_scores = s + router_bias.astype(jnp.float32)
        _, topk_idx = jax.lax.top_k(sel_scores, TOP_K)
        s_sel = jnp.take_along_axis(s, topk_idx, axis=1)
        denom = s_sel.sum(axis=1, keepdims=True)
        gates = jnp.where(denom > 1e-09, s_sel / (denom + 1e-09), 1.0 / TOP_K).astype(x.dtype)
        one_hot = jax.nn.one_hot(topk_idx, N_EXPERTS, dtype=x.dtype)
        comb = jnp.einsum('nke,nk->ne', one_hot, gates)
        h = jax.nn.gelu(jnp.einsum('nd,edh->neh', xf, ew1), approximate=False)
        y = jnp.einsum('neh,ehd->ned', h, ew2)
        routed_out = jnp.einsum('ned,ne->nd', y, comb)
        return (shared_out + routed_out).reshape(B, T, C)
    x = L0_attn_x
    x = _layernorm(x + _L0_attn_ref(x, L0_attn_Wq, L0_attn_bq, L0_attn_Wk, L0_attn_bk, L0_attn_Wv, L0_attn_bv, L0_attn_Wo, L0_attn_bo), axis=-1)
    x = _layernorm(x + _L0_ffn_ref(x, L0_ffn_router_w, L0_ffn_router_bias, L0_ffn_sw1, L0_ffn_sw3, L0_ffn_sw2, L0_ffn_ew1, L0_ffn_ew2), axis=-1)
    return x

_drawn_inputs = setup_inputs


def setup_inputs(seed=0):
    import zlib

    import numpy as np

    out = dict(_drawn_inputs(seed))
    spreads = {'L0_ffn_router_bias': (0.0, 0.1)}
    factors = {'L0_attn_Wq': 3.826, 'L0_attn_bq': 8.0, 'L0_attn_Wk': 4.031, 'L0_attn_bk': 8.0}
    for name, (base, spread) in spreads.items():
        noise = np.random.default_rng([zlib.crc32(name.encode()), seed]).standard_normal(out[name].shape)
        drawn = base * np.exp(spread * noise) if base else spread * noise
        out[name] = jnp.asarray(drawn.astype(out[name].dtype))
    for name, factor in factors.items():
        out[name] = (out[name] * factor).astype(out[name].dtype)
    return out
```

```python
from contextlib import ExitStack

import numpy as np

import concourse.bass as bass
from concourse import mybir

F32 = mybir.dt.float32
F32R = mybir.dt.float32r
ALU = mybir.AluOpType
ACT = mybir.ActivationFunctionType
AX = mybir.AxisListType

P = 128
NB, S = 8, 256
H, HD = 16, 8
TOK = NB * S
NTILE = TOK // P
GT = 512
NG = TOK // GT
TPG = GT // P
QT = S // P
NAB, NPAIR = 2, 8
HPS = 4
SPB = H // HPS
NSTEP = NB * SPB
LEAD = 6
NSLOT = 4
NE = 8
NSH = 2
VW = HD + 1
ROW0 = HD * NAB
SCALE = float(np.float32(1.0) / np.sqrt(np.float32(HD)))
EPS = 1e-5
W1, W3, E1, W2, E2, RW = 0, 256, 512, 512 + NE * P, 512 + NE * P + 256, 512 + 2 * NE * P + 256
WCOLS = RW + NE


def build_layer(nc, x, w_attn, b_cols, b_rows, w_ffn, out):
    ctx = ExitStack()
    with ctx:
        def sb(name, shape, dt=F32):
            return ctx.enter_context(nc.sbuf_tensor(name, shape, dt))

        def sem(name):
            return ctx.enter_context(nc.semaphore(name))

        gate_dram = nc.dram_tensor("gate_scratch", (NE, TOK), F32, kind="Internal").ap()

        wa = sb("wa", [P, 4, P])
        bqk = sb("bqk", [P, 2])
        bq_scaled = sb("bq_scaled", [P, 1])
        brow = sb("brow", [P, 2 * P + NE])
        wf = sb("wf", [P, WCOLS])
        wf_hi = sb("wf_hi", [P, RW], F32R)
        rw_parts = sb("rw_parts", [P, 2, NE], F32R)
        ident = sb("ident", [P, P])
        earlier = sb("earlier", [P, NE, NE])
        minus_half = sb("minus_half", [P, TPG])
        zero_col = sb("zero_col", [P, 1])
        zero_rows = sb("zero_rows", [2, 1, S], F32R)
        one_rows = sb("one_rows", [2, 1, S], F32R)

        xs = sb("xs", [P, NTILE, P])
        yt_hi = sb("yt_hi", [P, TOK], F32R)
        yt_lo = sb("yt_lo", [P, TOK], F32R)

        xt = sb("xt", [P, GT])
        qkf = sb("qkf", [P, 2, GT])
        qk_parts = sb("qk_parts", [P, 2 * 2 * 2 * GT], F32R)
        parts = qk_parts[:, :].rearrange("p (g i h t) -> p g i h t", g=2, i=2, h=2)
        wf_lo = qk_parts[:, 0:RW]
        qstack = sb("qstack", [P, NSLOT, NPAIR, S], F32R)
        kstack = sb("kstack", [P, NSLOT, NAB, NPAIR, S], F32R)
        v = sb("v", [P, NTILE, H, VW])
        top = sb("top", [P, QT, H])
        top_parts = sb("top_parts", [P, 2, QT, NAB, 2, NPAIR], F32R)
        top_rows = sb("top_rows", [NAB * 2 * NPAIR, 2, S], F32R)
        probs_mem = sb("probs_mem", [P, 4 * HPS * S])
        probs = probs_mem[:, :].rearrange("p (n j q) -> p n (j q)", n=4, j=HPS)
        att_raw = [sb("att_raw0", [P, SPB, S])[:, :, :], qkf[:, :, :].rearrange("p i (n q) -> p (i n) q", q=S)]
        rsum = sb("rsum", [P, H])
        att = xt[:, 0:S].rearrange("p (t d) -> p t d", t=QT)
        att_t = xt[:, S:2 * S]
        res1 = sb("res1", [P, QT, P])
        stats1 = sb("stats1", [P, QT, 6])
        mv1 = sb("mv1", [P, QT, 2])
        rstd1 = sb("rstd1", [P, QT])

        expl = sb("expl", [P, TPG, NE])
        sig = sb("sig", [P, TPG, NE])
        sel = sb("sel", [P, TPG, NE])
        diff = sb("diff", [P, TPG, NE, NE])
        tie = sb("tie", [P, TPG, NE, NE])
        rank = sb("rank", [P, TPG, NE])
        mask = sb("mask", [P, TPG, NE])
        picked = sb("picked", [P, TPG, NE])
        den = sb("den", [P, TPG])
        den_ok = sb("den_ok", [P, TPG])
        den_inv = sb("den_inv", [P, TPG])
        half = sb("half", [P, TPG])
        comb = sb("comb", [P, TPG, NE])
        comb_t = sb("comb_t", [NE, 2, S])

        sh_hi = kstack[:, 0, :, :, :].rearrange("p a r q -> p (a r q)").rearrange("p (j t) -> p j t", j=NSH)
        sh_lo = kstack[:, 1, :, :, :].rearrange("p a r q -> p (a r q)").rearrange("p (j t) -> p j t", j=NSH)
        gates = kstack[:, 2, :, :, :].rearrange("p a r q -> p (a r q)").rearrange("p (e t) -> p e t", e=NE)
        hid_hi = qstack[:, 0, :, :].rearrange("p r q -> p (r q)").rearrange("p (n t) -> p n t", n=4)
        hid_lo = qstack[:, 1, :, :].rearrange("p r q -> p (r q)").rearrange("p (n t) -> p n t", n=4)
        ffn = probs_mem[:, :].rearrange("p (n t) -> p n t", n=8)
        act_out, hid, acc_t = ffn[:, 0:2, :], ffn[:, 2:4, :], ffn[:, 4, :]
        res2 = ffn[:, 5, :].rearrange("p (t d) -> p t d", t=TPG)
        stats2 = ffn[:, 6, 0:6 * TPG].rearrange("p (t n) -> p t n", t=TPG)
        mv2 = ffn[:, 6, 64:64 + 2 * TPG].rearrange("p (t n) -> p t n", t=TPG)
        rstd2 = ffn[:, 6, 128:128 + TPG]

        wide = [ctx.enter_context(nc.psum_tensor(f"wide{i}", [P, 2, 512], F32)) for i in range(2)]
        max_bank = [ctx.enter_context(nc.psum_tensor(f"max_bank{i}", [P, 512], F32)) for i in range(2)]
        pv_bank = ctx.enter_context(nc.psum_tensor("pv_bank", [P, 512], F32))
        misc = ctx.enter_context(nc.psum_tensor("misc", [P, 512], F32))
        single = [wide[0][:, 0, :], wide[0][:, 1, :], wide[1][:, 0, :], wide[1][:, 1, :]]

        x_loaded = [sem(f"x_loaded{g}") for g in range(NG)]
        wa_loaded, bias_loaded, wf_loaded = sem("wa_loaded"), sem("bias_loaded"), sem("wf_loaded")
        ident_set, rows_set, zero_set = sem("ident_set"), sem("rows_set"), sem("zero_set")
        bq_set, v_ones_set, pv_cleared = sem("bq_set"), sem("v_ones_set"), sem("pv_cleared")
        q_cleared = [sem(f"q_cleared{i}") for i in range(NSLOT)]
        k_cleared = [sem(f"k_cleared{i}") for i in range(NSLOT)]
        pro_made, pro_act, v_made = sem("pro_made"), sem("pro_act"), sem("v_made")
        hi_split, parts_made = sem("hi_split"), sem("parts_made")
        ones_loaded = [sem(f"ones_loaded{i}") for i in range(NSLOT)]
        stack_loaded = [sem(f"stack_loaded{i}") for i in range(NSLOT)]
        shift_loaded = [sem(f"shift_loaded{i}") for i in range(2)]
        max_scores, max_taken, top_split = sem("max_scores"), sem("max_taken"), sem("top_split")
        scores_made, probs_made, pv_made, pv_taken = sem("scores_made"), sem("probs_made"), sem("pv_made"), sem("pv_taken")
        misc_made, misc_dve, misc_act = sem("misc_made"), sem("misc_dve"), sem("misc_act")
        dve_chain, pool_chain = sem("dve_chain"), sem("pool_chain")
        xb_made, stats_made, rstd_made, y_made = sem("xb_made"), sem("stats_made"), sem("rstd_made"), sem("y_made")
        route_dve, route_pool = sem("route_dve"), sem("route_pool")
        gate_stored, gates_loaded = [sem(f"gate_stored{i}") for i in range(2)], sem("gates_loaded")
        rw_split, w_split = sem("rw_split"), sem("w_split")
        up_made, act_made, hid_made, hi_made, lo_made, down_made = (
            sem("up_made"), sem("act_made"), sem("hid_made"), sem("hi_made"), sem("lo_made"), sem("down_made"))
        acc_taken, fin_made, fin_stats, fin_rstd, fin_out = (
            sem("acc_taken"), sem("fin_made"), sem("fin_stats"), sem("fin_rstd"), sem("fin_out"))
        out_stored = sem("out_stored")

        UP0 = NSTEP
        EX0 = UP0 + NG * NSH
        NEX = NG * NE
        LAG = 3
        LAST = EX0 + NEX + LAG + 5
        jobs = {t: [] for t in range(-LEAD, LAST)}

        for g in range(1, NG):
            jobs[g - LEAD].append(("project", g))
        for b in range(NB):
            jobs[SPB * b - 2].append(("shift", b))
            first = SPB * (b + 1)
            for kind, when in (("norm0", 1), ("norm1", 1), ("attT", 2), ("wo", 3), ("yT", 4)):
                jobs[first + when].append((kind, b))
            late = 2 if b // 2 == NG - 1 else 0
            router = EX0 if late else first + 5
            jobs[router].append(("router", b))
            if b % 2:
                for i in range(3):
                    jobs[router + i].append((f"route{i}", b // 2))
                jobs[router + 3 + late] += [("combT", b - 1), ("combT", b)]
        for n in range(NG * NSH):
            jobs[UP0 + n].append(("shared", n))
        for m in range(NEX):
            jobs[EX0 + m].append(("expert", m))
            jobs[EX0 + m + LAG].append(("down", m))
            if m % NE == NE - 1:
                g = m // NE
                for i, kind in enumerate(("accT", "finT", "norm2")):
                    jobs[EX0 + m + LAG + 1 + i].append((kind, g))
        TICKS = range(-LEAD, LAST)

        def step(t):
            return 0 <= t < NSTEP

        TAKER = {"norm0": "dve", "norm1": "dve", "wo": "dve", "attT": "act", "yT": "both", "router": "act",
                 "shift": "act", "combT": "act"}
        uses = [u for t in TICKS for u in jobs[t] if u[0] in TAKER]
        made = {u: i + 1 for i, u in enumerate(uses)}
        taken, by_act, by_dve = {}, 0, 0
        for u in uses:
            by_act += TAKER[u[0]] in ("act", "both")
            by_dve += TAKER[u[0]] in ("dve", "both")
            taken[u] = (by_act, by_dve)

        def slot_loads(b):
            return 16 * (9 * (b // NSLOT + 1) + 2 * (b // NSLOT))

        def link(eng, chain, count, ins):
            count[0] += 1
            ins.then_inc(chain, 1)
            eng.wait_ge(chain, count[0])

        def tokens(g):
            return slice(g * GT, (g + 1) * GT)

        def tiles(g):
            return slice(g * TPG, (g + 1) * TPG)

        block = ctx.enter_context(nc.Block())

        @block.sync
        def _(sp):
            xg = x.rearrange("b (t p) d -> p (b t) d", p=P)
            outg = out.rearrange("b (t p) d -> p (b t) d", p=P)
            sp.dma_start(xs[:, tiles(0), :], xg[:, tiles(0), :]).then_inc(x_loaded[0], 16)
            sp.dma_start(bqk[:, :], b_cols).then_inc(bias_loaded, 16)
            sp.dma_start(brow[:, :], b_rows.to_broadcast([P, 2 * P + NE])).then_inc(bias_loaded, 16)
            for g in range(1, NG):
                sp.dma_start(xs[:, tiles(g), :], xg[:, tiles(g), :]).then_inc(x_loaded[g], 16)

            def move(dst, src):
                return sp.dma_start(dst.bitcast(F32), src.bitcast(F32))

            def ones(b):
                sp.wait_ge(rows_set, 2)
                sp.wait_ge(k_cleared[b], 1)
                for ab in range(NAB):
                    move(kstack[32 * ab:32 * ab + 2, b, ab, :, :],
                                 one_rows[:, :, :].to_broadcast([2, NPAIR, S])).then_inc(ones_loaded[b], 16)

            def stack(b):
                s, g, t0 = b % NSLOT, b // 2, (b % 2) * S
                par = g % 2
                if b < NSLOT:
                    ones(b)
                    sp.wait_ge(q_cleared[s], 1)
                else:
                    sp.wait_ge(scores_made, 2 * SPB * (b - NSLOT + 1))
                    for r in (0, 32):
                        move(qstack[r:r + 2, s, :, :],
                                     zero_rows[:, :, :].to_broadcast([2, NPAIR, S])).then_inc(stack_loaded[s], 16)
                sp.wait_ge(parts_made, 2 * g + 1)
                for i, part in enumerate((0, 0, 1)):
                    r = 32 * i + ROW0
                    move(qstack[r:r + NAB * HD, s, :, :],
                                 parts[:, par, 0, part, t0:t0 + S]).then_inc(stack_loaded[s], 16)
                sp.wait_ge(parts_made, 2 * g + 2)
                for i, part in enumerate((0, 1, 0)):
                    for ab in range(NAB):
                        r = 32 * i + ROW0 + HD * ab
                        move(kstack[r:r + HD, s, ab, :, :],
                                     parts[64 * ab:64 * ab + 64, par, 1, part, t0:t0 + S]).then_inc(stack_loaded[s], 16)

            def load_gates(g):
                if g == 0:
                    sp.wait_ge(scores_made, 2 * NSTEP)
                else:
                    sp.wait_ge(hid_made, NG * NSH + NE * g)
                for i in range(2):
                    sp.wait_ge(gate_stored[i], 16 * (g + 1))
                src = gate_dram.rearrange("(o e) t -> o e t", o=1)[:, :, tokens(g)]
                sp.dma_start(gates.bitcast(F32), src.to_broadcast([P, NE, GT])).then_inc(gates_loaded, 16)

            for b in range(3):
                stack(b)
            for tick in TICKS:
                for kind, b in jobs[tick]:
                    if kind == "shift":
                        sp.wait_ge(misc_act, taken["shift", b][0])
                        for ab in range(NAB):
                            move(qstack[32 * ab:32 * ab + 2, b % NSLOT, :, :],
                                         top_rows[16 * ab:16 * ab + 16, b % 2, :]).then_inc(shift_loaded[b % 2], 16)
                        if b == 0:
                            stack(3)
                    if kind == "combT":
                        sp.wait_ge(misc_act, taken["combT", b][0])
                        sp.dma_start(gate_dram[:, b * S:(b + 1) * S], comb_t[:, b % 2, :]).then_inc(gate_stored[b % 2], 16)
                    if kind == "norm2":
                        sp.wait_ge(fin_out, b + 1)
                        sp.dma_start(outg[:, tiles(b), :], xs[:, tiles(b), :]).then_inc(out_stored, 16)
                    if kind == "expert" and b % NE == NE - 1 and b < NEX - 1:
                        load_gates(b // NE + 1)
                if tick == UP0 + 2:
                    load_gates(0)
                if step(tick) and tick % SPB == 3 and tick // SPB + NSLOT < NB:
                    stack(tick // SPB + NSLOT)
            sp.wait_ge(out_stored, 16 * NG)

        @block.gpsimd
        def _(pool):
            cnt = [0]

            def chain(ins):
                link(pool, pool_chain, cnt, ins)

            chain(pool.memset(ident[:, :], 0.0))
            pool.affine_select(out=ident[:, :], in_=ident[:, :], compare_op=ALU.not_equal, fill=1.0, base=0,
                               pattern=[[-1, P]], channel_multiplier=1).then_inc(ident_set, 1)
            pool.memset(one_rows[:, :, :].bitcast(F32), 1.0).then_inc(rows_set, 1)
            pool.memset(zero_rows[:, :, :].bitcast(F32), 0.0).then_inc(rows_set, 1)
            pool.wait_ge(bias_loaded, 32)
            pool.tensor_scalar(bq_scaled[:, :], bqk[:, 0:1], SCALE, None, ALU.mult).then_inc(bq_set, 1)
            chain(pool.memset(minus_half[:, :], -0.5))
            chain(pool.memset(earlier[:, :, :], 1.0))
            chain(pool.affine_select(out=earlier[:, :, :], in_=earlier[:, :, :], compare_op=ALU.is_gt, fill=0.0, base=0,
                                     pattern=[[1, NE], [-1, NE]], channel_multiplier=0))

            def split(g):
                par = g % 2
                for i in range(2):
                    pool.wait_ge(pro_act, 3 * g + 2 + i)
                    if g >= 2 and i == 0:
                        for b in (2 * g - 4, 2 * g - 3):
                            pool.wait_ge(stack_loaded[b % NSLOT], slot_loads(b))
                    pool.tensor_scalar(parts[:, par, i, 0, :], qkf[:, i, :], 1.0, None, ALU.mult).then_inc(hi_split, 1)
                    pool.wait_ge(hi_split, 2 * g + i + 1)
                    pool.tensor_tensor(parts[:, par, i, 1, :], qkf[:, i, :], parts[:, par, i, 0, :].bitcast(F32),
                                       ALU.subtract).then_inc(parts_made, 1)

            def add_bo(g):
                pool.wait_ge(pro_made, 4 * g + 1)
                pool.tensor_tensor(xs[:, tiles(g), :], xs[:, tiles(g), :],
                                   brow[:, None, P:2 * P].to_broadcast([P, TPG, P]), ALU.add).then_inc(xb_made, 1)

            def split_weights(lo, hi):
                chain(pool.tensor_scalar(wf_hi[:, lo:hi], wf[:, lo:hi], 1.0, None, ALU.mult))
                return pool.tensor_tensor(wf_lo[:, lo:hi], wf[:, lo:hi], wf_hi[:, lo:hi].bitcast(F32), ALU.subtract)

            split(0)
            split(1)
            add_bo(0)
            pool.wait_ge(wf_loaded, 16)
            chain(pool.tensor_scalar(rw_parts[:, 0, :], wf[:, RW:], 1.0, None, ALU.mult))
            pool.tensor_tensor(rw_parts[:, 1, :], wf[:, RW:], rw_parts[:, 0, :].bitcast(F32),
                               ALU.subtract).then_inc(rw_split, 1)
            split(2)
            for g in range(1, NG):
                add_bo(g)
            CUT = RW // 8
            cuts = [(c, c + CUT) for c in range(0, RW, CUT)]

            for tick in TICKS:
                if tick == 1:
                    split(3)
                if tick == SPB * (NB - NSLOT):
                    for b in range(NSLOT, NB):
                        pool.wait_ge(stack_loaded[b % NSLOT], slot_loads(b))
                if tick >= SPB * (NB - NSLOT) and cuts:
                    ins = split_weights(*cuts.pop(0))
                    if cuts:
                        chain(ins)
                    else:
                        ins.then_inc(w_split, 1)
                for kind, n in jobs[tick]:
                    if kind == "wo":
                        pool.wait_ge(stats_made, n + 1)
                        chain(pool.tensor_scalar(rstd1[:, :], mv1[:, :, 1], EPS, None, ALU.add))
                        pool.tensor_tensor(rstd1[:, :], rstd1[:, :], minus_half[:, 0:QT], ALU.pow).then_inc(rstd_made, 1)
                    if kind == "route0":
                        pool.wait_ge(misc_act, taken["router", 2 * n + 1][0])
                        pool.tensor_scalar(expl[:, :, :], expl[:, :, :], 1.0, None, ALU.add).then_inc(route_pool, 1)
                        pool.wait_ge(route_dve, 3 * n + 1)
                        chain(pool.tensor_tensor(sel[:, :, :], sig[:, :, :],
                                                 brow[:, None, 2 * P:].to_broadcast([P, TPG, NE]), ALU.add))
                        for t in range(TPG):
                            ins = pool.tensor_tensor(diff[:, t, :, :], sel[:, t, None, :].to_broadcast([P, NE, NE]),
                                                     sel[:, t, :, None].to_broadcast([P, NE, NE]), ALU.subtract)
                        chain(ins)
                        pool.tensor_scalar(tie[:, :, :, :], diff[:, :, :, :], 0.0, None, ALU.is_equal)
                        chain(pool.tensor_scalar(diff[:, :, :, :], diff[:, :, :, :], 0.0, None, ALU.is_gt))
                        for t in range(TPG):
                            ins = pool.tensor_tensor(tie[:, t, :, :], tie[:, t, :, :], earlier[:, :, :], ALU.mult)
                        chain(ins)
                        pool.tensor_tensor(diff[:, :, :, :], diff[:, :, :, :], tie[:, :, :, :],
                                           ALU.add).then_inc(route_pool, 1)
                    if kind == "route1":
                        pool.wait_ge(route_dve, 3 * n + 2)
                        chain(pool.tensor_scalar(mask[:, :, :], rank[:, :, :], 1.5, None, ALU.is_lt))
                        pool.tensor_tensor(picked[:, :, :], mask[:, :, :], sig[:, :, :], ALU.mult).then_inc(route_pool, 1)
                    if kind == "route2":
                        pool.wait_ge(route_dve, 3 * n + 3)
                        chain(pool.tensor_scalar(den_ok[:, :], den[:, :], 1e-9, None, ALU.is_gt))
                        chain(pool.tensor_scalar(half[:, :], den_ok[:, :], -0.5, 0.5, ALU.mult, ALU.add))
                        chain(pool.tensor_tensor(den_inv[:, :], den_inv[:, :], den_ok[:, :], ALU.mult))
                        chain(pool.tensor_tensor(picked[:, :, :], picked[:, :, :],
                                                 den_inv[:, :, None].to_broadcast([P, TPG, NE]), ALU.mult))
                        chain(pool.tensor_tensor(mask[:, :, :], mask[:, :, :],
                                                 half[:, :, None].to_broadcast([P, TPG, NE]), ALU.mult))
                        if n:
                            pool.wait_ge(misc_made, made["combT", 2 * n - 1])
                        pool.tensor_tensor(comb[:, :, :], picked[:, :, :], mask[:, :, :], ALU.add).then_inc(route_pool, 1)
                    if kind == "shared":
                        pool.wait_ge(hid_made, n + 1)
                        pool.tensor_scalar(sh_hi[:, n % NSH, tokens(n // NSH)], hid[:, n % 2, :], 1.0, None,
                                           ALU.mult).then_inc(hi_made, 1)
                    if kind == "expert":
                        pool.wait_ge(hid_made, NG * NSH + n + 1)
                        if n >= 4:
                            pool.wait_ge(down_made, n - 3)
                        pool.tensor_scalar(hid_hi[:, n % 4, :], hid[:, n % 2, :], 1.0, None, ALU.mult).then_inc(hi_made, 1)
                    if kind == "finT":
                        pool.wait_ge(fin_stats, n + 1)
                        chain(pool.tensor_scalar(rstd2, mv2[:, :, 1], EPS, None, ALU.add))
                        pool.tensor_tensor(rstd2, rstd2, minus_half[:, :], ALU.pow).then_inc(fin_rstd, 1)

        @block.scalar
        def _(act):
            act.dma_start(wa[:, :, :], w_attn).then_inc(wa_loaded, 16)
            act.dma_start(wf[:, :], w_ffn).then_inc(wf_loaded, 16)
            act.wait_ge(zero_set, 1)

            def clear(tile, n, cleared):
                nc.scalar.copy(tile, zero_col[:, :].to_broadcast([P, n])).then_inc(cleared, 1)

            def clear_q(s):
                clear(qstack[:, s, :, :].rearrange("p r q -> p (r q)"), NPAIR * S, q_cleared[s])

            def clear_k(s):
                clear(kstack[:, s, :, :, :].rearrange("p a r q -> p (a r q)"), NAB * NPAIR * S, k_cleared[s])

            def project(g):
                act.wait_ge(pro_made, 4 * g + 1)
                nc.scalar.copy(xt[:, :], single[0]).then_inc(pro_act, 1)
                act.wait_ge(pro_made, 4 * g + 2)
                if g == 0:
                    act.wait_ge(bq_set, 1)
                else:
                    act.wait_ge(parts_made, 2 * g - 1)
                nc.scalar.activation(qkf[:, 0, :], single[1], ACT.Identity, bias=bq_scaled[:, 0:1],
                                     scale=SCALE).then_inc(pro_act, 1)
                act.wait_ge(pro_made, 4 * g + 3)
                if g:
                    act.wait_ge(parts_made, 2 * g)
                nc.scalar.activation(qkf[:, 1, :], single[2], ACT.Identity, bias=bqk[:, 1:2]).then_inc(pro_act, 1)

            clear_q(0)
            project(0)
            clear_q(2)
            clear_k(2)
            for tick in TICKS:
                if step(tick):
                    for kt in range(QT):
                        k = 2 * tick + kt
                        act.wait_ge(scores_made, k + 1)
                        if tick >= 2:
                            act.wait_ge(pv_made, tick - 1)
                        nc.scalar.activation(probs[:, k % 4, :], wide[k % 2][:, :, :].rearrange("p a b -> p (a b)"),
                                             ACT.Exp).then_inc(probs_made, 1)
                if step(tick - 1):
                    i = tick - 1
                    act.wait_ge(pv_made, i + 1)
                    if i == SPB:
                        act.wait_ge(parts_made, 2 * NG)
                    nc.scalar.copy(att_raw[i // SPB % 2][:, i % SPB, :], pv_bank[:, 0:S]).then_inc(pv_taken, 1)
                for kind, b in jobs[tick]:
                    if TAKER.get(kind) in ("act", "both"):
                        act.wait_ge(misc_made, made[kind, b])
                    if kind == "project":
                        project(b)
                        if b == 2:
                            clear_q(3)
                            clear_k(3)
                    if kind == "shift":
                        if b >= 2:
                            act.wait_ge(shift_loaded[b % 2], 32 * (b // 2))
                        nc.scalar.copy(top_rows[:, b % 2, :], misc[0:NAB * 2 * NPAIR, 0:S]).then_inc(misc_act, 1)
                    if kind == "attT":
                        nc.scalar.copy(att_t, misc[:, 0:S]).then_inc(misc_act, 1)
                    if kind == "yT":
                        nc.scalar.copy(yt_hi[:, b * S:(b + 1) * S], misc[:, 0:S]).then_inc(misc_act, 1)
                    if kind == "router":
                        if b % 2 == 0 and b:
                            act.wait_ge(route_pool, 2 * b)
                        nc.scalar.activation(expl[:, QT * (b % 2):QT * (b % 2) + QT, :],
                                             misc[:, 0:QT * NE].rearrange("p (t e) -> p t e", e=NE), ACT.Exp,
                                             scale=-1.0).then_inc(misc_act, 1)
                    if kind == "combT":
                        if b >= 2:
                            act.wait_ge(gate_stored[b % 2], 16 * (b // 2))
                        nc.scalar.copy(comb_t[:, b % 2, :], misc[0:NE, 0:S]).then_inc(misc_act, 1)
                    if kind == "shared":
                        act.wait_ge(up_made, b + 1)
                        if b >= 2:
                            act.wait_ge(hid_made, b - 1)
                        nc.scalar.activation(act_out[:, b % 2, :], wide[b % 2][:, 0, :], ACT.Silu).then_inc(act_made, 1)
                    if kind == "expert":
                        n = NG * NSH + b
                        act.wait_ge(up_made, n + 1)
                        act.wait_ge(hid_made, n - 1)
                        nc.scalar.activation(act_out[:, n % 2, :], single[b % 4], ACT.Gelu).then_inc(act_made, 1)
                    if kind == "accT":
                        act.wait_ge(down_made, NE * (b + 1))
                        if b:
                            act.wait_ge(fin_made, b)
                        nc.scalar.copy(acc_t, max_bank[b % 2][:, :]).then_inc(acc_taken, 1)

        @block.vector
        def _(dve):
            cnt = [0]

            def chain(ins):
                link(dve, dve_chain, cnt, ins)

            dve.memset(zero_col[:, :], 0.0).then_inc(zero_set, 1)
            dve.memset(v[:, :, :, HD:VW], 1.0).then_inc(v_ones_set, 1)
            dve.memset(kstack[:, 0, :, :, :].bitcast(F32), 0.0).then_inc(k_cleared[0], 1)
            dve.memset(pv_bank[:, :], 0.0).then_inc(pv_cleared, 1)
            dve.memset(qstack[:, 1, :, :].bitcast(F32), 0.0).then_inc(q_cleared[1], 1)
            dve.memset(kstack[:, 1, :, :, :].bitcast(F32), 0.0).then_inc(k_cleared[1], 1)

            def project_v(g):
                dve.wait_ge(pro_made, 4 * g + 4)
                if g == 0:
                    dve.wait_ge(bias_loaded, 32)
                for t in range(TPG):
                    ins = dve.tensor_tensor(v[:, g * TPG + t, :, 0:HD],
                                            single[3][:, t * P:(t + 1) * P].rearrange("p (h d) -> p h d", h=H),
                                            brow[:, 0:P].rearrange("p (h d) -> p h d", h=H), ALU.add)
                ins.then_inc(v_made, 1)

            project_v(0)
            for tick in TICKS:
                if step(tick + LEAD):
                    i = tick + LEAD
                    b, h0 = i // SPB, i % SPB * HPS
                    if i % SPB == 0 and b:
                        dve.wait_ge(top_split, b)
                    for c in range(4):
                        qt, h = c // 2, h0 + 2 * (c % 2)
                        dve.wait_ge(max_scores, 4 * i + c + 1)
                        dve.tensor_reduce(top[:, qt, h:h + 2],
                                          max_bank[c % 2][:, :].rearrange("p (h k) -> p h k", h=2), AX.X,
                                          ALU.max).then_inc(max_taken, 1)
                    if i % SPB == SPB - 1:
                        dve.wait_ge(max_taken, 4 * (i + 1))
                        if b >= 2:
                            dve.wait_ge(misc_made, made["shift", b - 2])
                        tops = top[:, :, :].rearrange("p q (a r) -> p q a r", a=NAB)
                        hi, lo = (top_parts[:, b % 2, :, :, n, :] for n in range(2))
                        chain(dve.tensor_scalar(hi, tops, -1.0, None, ALU.mult))
                        dve.scalar_tensor_tensor(out=lo, in0=tops, scalar=-1.0, in1=hi.bitcast(F32), op0=ALU.mult,
                                                 op1=ALU.subtract).then_inc(top_split, 1)
                for kind, b in jobs[tick]:
                    if kind == "project":
                        project_v(b)
                    if kind in ("norm0", "norm1"):
                        qt = int(kind[-1])
                        dve.wait_ge(misc_made, made[kind, b])
                        heads = misc[:, :].rearrange("p (h r) -> p h r", h=H)
                        chain(dve.reciprocal(rsum[:, :], heads[:, :, HD]))
                        dve.tensor_tensor(att[:, qt, :].rearrange("p (h d) -> p h d", h=H), heads[:, :, 0:HD],
                                          rsum[:, :, None].to_broadcast([P, H, HD]), ALU.mult).then_inc(misc_dve, 1)
                    if kind == "wo":
                        dve.wait_ge(misc_made, made[kind, b])
                        dve.wait_ge(xb_made, b // 2 + 1)
                        ins = dve.tensor_tensor(res1[:, :, :], misc[:, 0:S].rearrange("p (t d) -> p t d", t=QT),
                                                xs[:, QT * b:QT * b + QT, :], ALU.add).then_inc(misc_dve, 1)
                        dve.wait_ge(misc_dve, taken[kind, b][1])
                        for t in range(QT):
                            ins = dve.bn_stats(stats1[:, t, :], res1[:, t, :])
                        chain(ins)
                        for t in range(QT):
                            ins = dve.bn_aggr(mv1[:, t, :], stats1[:, t, :])
                        ins.then_inc(stats_made, 1)
                    if kind == "yT":
                        dve.wait_ge(rstd_made, b + 1)
                        for t in range(QT):
                            ins = dve.tensor_scalar(xs[:, QT * b + t, :], res1[:, t, :], mv1[:, t, 0:1],
                                                    rstd1[:, t:t + 1], ALU.subtract, ALU.mult)
                        ins.then_inc(y_made, 1)
                        dve.wait_ge(misc_act, taken[kind, b][0])
                        dve.tensor_tensor(yt_lo[:, b * S:(b + 1) * S], misc[:, 0:S],
                                          yt_hi[:, b * S:(b + 1) * S].bitcast(F32), ALU.subtract).then_inc(misc_dve, 1)
                    if kind == "route0":
                        dve.wait_ge(route_pool, 4 * b + 1)
                        dve.reciprocal(sig[:, :, :], expl[:, :, :]).then_inc(route_dve, 1)
                    if kind == "route1":
                        dve.wait_ge(route_pool, 4 * b + 2)
                        dve.tensor_reduce(rank[:, :, :], diff[:, :, :, :], AX.X, ALU.add).then_inc(route_dve, 1)
                    if kind == "route2":
                        dve.wait_ge(route_pool, 4 * b + 3)
                        chain(dve.tensor_reduce(den[:, :], picked[:, :, :], AX.X, ALU.add))
                        chain(dve.tensor_scalar(den_inv[:, :], den[:, :], 1e-9, None, ALU.add))
                        dve.reciprocal(den_inv[:, :], den_inv[:, :]).then_inc(route_dve, 1)
                    if kind == "shared":
                        n = b
                        dve.wait_ge(act_made, n + 1)
                        if n >= 2:
                            dve.wait_ge(lo_made, n - 1)
                        dve.tensor_tensor(hid[:, n % 2, :], act_out[:, n % 2, :], wide[n % 2][:, 1, :],
                                          ALU.mult).then_inc(hid_made, 1)
                        dve.wait_ge(hi_made, n + 1)
                        dve.tensor_tensor(sh_lo[:, n % NSH, tokens(n // NSH)], hid[:, n % 2, :],
                                          sh_hi[:, n % NSH, tokens(n // NSH)].bitcast(F32), ALU.subtract).then_inc(lo_made, 1)
                    if kind == "expert":
                        n = NG * NSH + b
                        dve.wait_ge(act_made, n + 1)
                        if n >= 2:
                            dve.wait_ge(lo_made, n - 1)
                        dve.wait_ge(gates_loaded, 16 * (b // NE + 1))
                        dve.tensor_tensor(hid[:, n % 2, :], act_out[:, n % 2, :], gates[:, b % NE, :].bitcast(F32),
                                          ALU.mult).then_inc(hid_made, 1)
                    if kind in ("expert", "down"):
                        m = b - 1 if kind == "expert" else b
                        last = kind == "down" and b == NEX - LAG
                        if (kind == "expert" and b) or last:
                            m = b - 1 if kind == "expert" else NEX - 1
                            n = NG * NSH + m
                            dve.wait_ge(hi_made, n + 1)
                            dve.tensor_tensor(hid_lo[:, m % 4, :], hid[:, n % 2, :], hid_hi[:, m % 4, :].bitcast(F32),
                                              ALU.subtract).then_inc(lo_made, 1)
                    if kind == "finT":
                        dve.wait_ge(fin_made, b + 1)
                        chain(dve.tensor_tensor(res2, pv_bank[:, :].rearrange("p (t d) -> p t d", t=TPG),
                                                xs[:, tiles(b), :], ALU.add))
                        for t in range(TPG):
                            ins = dve.bn_stats(stats2[:, t, :], res2[:, t, :])
                        chain(ins)
                        for t in range(TPG):
                            ins = dve.bn_aggr(mv2[:, t, :], stats2[:, t, :])
                        ins.then_inc(fin_stats, 1)
                    if kind == "norm2":
                        dve.wait_ge(fin_rstd, b + 1)
                        for t in range(TPG):
                            ins = dve.tensor_scalar(xs[:, b * TPG + t, :], res2[:, t, :], mv2[:, t, 0:1],
                                                    rstd2[:, t:t + 1], ALU.subtract, ALU.mult)
                        ins.then_inc(fin_out, 1)

        @block.tensor
        def _(pe):
            mm = nc.tensor.matmul

            def project(g):
                pe.wait_ge(x_loaded[g], 16)
                for t in range(TPG):
                    ins = nc.tensor.transpose(single[0][:, t * P:(t + 1) * P], xs[:, g * TPG + t, :], ident[:, :])
                ins.then_inc(pro_made, 1)
                pe.wait_ge(pro_act, 3 * g + 1)
                if g == 0:
                    pe.wait_ge(wa_loaded, 16)
                for i in range(2):
                    mm(single[1 + i], wa[:, i, :], xt[:, :], start=True, stop=True).then_inc(pro_made, 1)
                if g:
                    pe.wait_ge(v_made, g)
                for t in range(TPG):
                    ins = mm(single[3][:, t * P:(t + 1) * P], xt[:, t * P:(t + 1) * P], wa[:, 2, :],
                             start=True, stop=True)
                ins.then_inc(pro_made, 1)

            def three(out_ap, w_hi, w_lo, m_hi, m_lo, first, last):
                mm(out_ap, w_lo, m_hi, start=first, stop=False)
                mm(out_ap, w_hi, m_lo, start=False, stop=False)
                return mm(out_ap, w_hi, m_hi, start=False, stop=last)

            def maxima(i):
                b, h0 = i // SPB, i % SPB * HPS
                s = b % NSLOT
                if i % SPB == 0:
                    pe.wait_ge(stack_loaded[s], slot_loads(b))
                    pe.wait_ge(ones_loaded[s], 32)
                for c in range(4):
                    qt, h1 = c // 2, h0 + 2 * (c % 2)
                    if 4 * i + c >= 2:
                        pe.wait_ge(max_taken, 4 * i + c - 1)
                    for j in range(2):
                        ab, r = divmod(h1 + j, NPAIR)
                        ins = mm(max_bank[c % 2][:, j * S:(j + 1) * S], qstack[:, s, r, qt * P:(qt + 1) * P],
                                 kstack[:, s, ab, r, :], start=True, stop=True)
                    ins.then_inc(max_scores, 1)

            def scores(i):
                b, h0 = i // SPB, i % SPB * HPS
                s = b % NSLOT
                if i % SPB == 0:
                    pe.wait_ge(shift_loaded[b % 2], 32 * (b // 2 + 1))
                if i == 0:
                    pe.wait_ge(pro_act, 3 * NG)
                    pe.wait_ge(v_made, NG)
                for kt in range(QT):
                    if i >= 1:
                        pe.wait_ge(probs_made, 2 * i + kt - 1)
                    for j in range(HPS):
                        ab, r = divmod(h0 + j, NPAIR)
                        ins = mm(wide[kt][:, j // 2, j % 2 * S:(j % 2 + 1) * S], kstack[:, s, ab, r, kt * P:(kt + 1) * P],
                                 qstack[:, s, r, :], start=True, stop=True)
                    ins.then_inc(scores_made, 1)

            def times_v(i):
                b, h0 = i // SPB, i % SPB * HPS
                if i == 0:
                    pe.wait_ge(v_ones_set, 1)
                    pe.wait_ge(pv_cleared, 1)
                else:
                    pe.wait_ge(pv_taken, i)
                for kt in range(QT):
                    pe.wait_ge(probs_made, 2 * i + kt + 1)
                    for j in range(HPS):
                        ins = mm(pv_bank[32 * j:32 * j + VW, 0:S], v[:, QT * b + kt, h0 + j, :],
                                 probs[:, (2 * i + kt) % 4, j * S:(j + 1) * S], start=(kt == 0), stop=(kt == QT - 1))
                ins.then_inc(pv_made, 1)

            pe.wait_ge(ident_set, 1)
            project(0)
            for tick in TICKS:
                if step(tick):
                    scores(tick)
                if step(tick + LEAD):
                    maxima(tick + LEAD)
                if step(tick - 1):
                    times_v(tick - 1)
                for kind, b in jobs[tick]:
                    if kind in TAKER and made[kind, b] > 1:
                        before = taken[uses[made[kind, b] - 2]]
                        if before[0]:
                            pe.wait_ge(misc_act, before[0])
                        if before[1]:
                            pe.wait_ge(misc_dve, before[1])
                    if kind == "project":
                        project(b)
                    if kind == "shift":
                        pe.wait_ge(top_split, b + 1)
                        for t in range(QT):
                            ins = nc.tensor.transpose(
                                misc[0:NAB * 2 * NPAIR, t * P:(t + 1) * P],
                                top_parts[:, b % 2, t, :, :, :].rearrange("p a n r -> p (a n r)").bitcast(F32), ident[:, :])
                        ins.then_inc(misc_made, 1)
                    if kind in ("norm0", "norm1"):
                        t = int(kind[-1])
                        pe.wait_ge(pv_taken, SPB * (b + 1))
                        for n in range(SPB):
                            ins = nc.tensor.transpose(misc[:, n * P:(n + 1) * P],
                                                      att_raw[b % 2][:, n, t * P:(t + 1) * P], ident[:, :])
                        ins.then_inc(misc_made, 1)
                    if kind == "attT":
                        for t in range(QT):
                            ins = nc.tensor.transpose(misc[:, t * P:(t + 1) * P], att[:, t, :], ident[:, :])
                        ins.then_inc(misc_made, 1)
                    if kind == "wo":
                        pe.wait_ge(misc_act, taken["attT", b][0])
                        for t in range(QT):
                            ins = mm(misc[:, t * P:(t + 1) * P], att_t[:, t * P:(t + 1) * P], wa[:, 3, :],
                                     start=True, stop=True)
                        ins.then_inc(misc_made, 1)
                    if kind == "yT":
                        pe.wait_ge(y_made, b + 1)
                        for t in range(QT):
                            ins = nc.tensor.transpose(misc[:, t * P:(t + 1) * P], xs[:, QT * b + t, :], ident[:, :])
                        ins.then_inc(misc_made, 1)
                    if kind == "router":
                        pe.wait_ge(rw_split, 1)
                        pe.wait_ge(misc_dve, taken["yT", b][1])
                        for t in range(QT):
                            tok = slice((QT * b + t) * P, (QT * b + t + 1) * P)
                            ins = three(misc[:, t * NE:(t + 1) * NE], yt_hi[:, tok], yt_lo[:, tok],
                                        rw_parts[:, 0, :], rw_parts[:, 1, :], True, True)
                        ins.then_inc(misc_made, 1)
                    if kind == "combT":
                        pe.wait_ge(route_pool, 4 * (b // 2) + 4)
                        for t in range(QT):
                            ins = nc.tensor.transpose(misc[0:NE, t * P:(t + 1) * P], comb[:, QT * (b % 2) + t, :], ident[:, :])
                        ins.then_inc(misc_made, 1)
                    if kind == "shared":
                        g, j = divmod(b, NSH)
                        if b < 2:
                            pe.wait_ge(probs_made, 2 * NSTEP)
                            pe.wait_ge(w_split, 1)
                        else:
                            pe.wait_ge(hid_made, b - 1)
                        pe.wait_ge(misc_dve, taken["yT", 2 * g + 1][1])
                        for n, w in enumerate((W1, W3)):
                            c = slice(w + j * P, w + (j + 1) * P)
                            ins = three(wide[b % 2][:, n, :], wf_hi[:, c], wf_lo[:, c], yt_hi[:, tokens(g)],
                                        yt_lo[:, tokens(g)], True, True)
                        ins.then_inc(up_made, 1)
                    if kind == "expert":
                        g, e = divmod(b, NE)
                        if b < 4:
                            pe.wait_ge(hid_made, NG * NSH - 1 + b // 2)
                        else:
                            pe.wait_ge(act_made, NG * NSH + b - 3)
                        c = slice(E1 + e * P, E1 + (e + 1) * P)
                        three(single[b % 4], wf_hi[:, c], wf_lo[:, c], yt_hi[:, tokens(g)], yt_lo[:, tokens(g)],
                              True, True).then_inc(up_made, 1)
                    if kind == "down":
                        g, e = divmod(b, NE)
                        acc = max_bank[g % 2][:, :]
                        if e == 0:
                            pe.wait_ge(max_taken, 4 * NSTEP)
                            if g >= 2:
                                pe.wait_ge(acc_taken, g - 1)
                            pe.wait_ge(lo_made, NSH * (g + 1))
                            for j in range(NSH):
                                c = slice(W2 + j * P, W2 + (j + 1) * P)
                                three(acc, wf_hi[:, c], wf_lo[:, c], sh_hi[:, j, tokens(g)], sh_lo[:, j, tokens(g)],
                                      j == 0, False)
                        pe.wait_ge(lo_made, NG * NSH + b + 1)
                        c = slice(E2 + e * P, E2 + (e + 1) * P)
                        three(acc, wf_hi[:, c], wf_lo[:, c], hid_hi[:, b % 4, :], hid_lo[:, b % 4, :],
                              False, e == NE - 1).then_inc(down_made, 1)
                    if kind == "finT":
                        pe.wait_ge(acc_taken, b + 1)
                        if b:
                            pe.wait_ge(fin_stats, b)
                        for t in range(TPG):
                            ins = nc.tensor.transpose(pv_bank[:, t * P:(t + 1) * P], acc_t[:, t * P:(t + 1) * P], ident[:, :])
                        ins.then_inc(fin_made, 1)


_ARGS = ("x", "w_attn", "b_cols", "b_rows", "w_ffn")


def lay_out(i):
    def by_ab_d_pair(w):
        return w.reshape(-1, NAB, NPAIR, HD).transpose(0, 1, 3, 2).reshape(w.shape)

    wq, wk = (by_ab_d_pair(np.asarray(i[f"L0_attn_W{n}"])) for n in "qk")
    w_attn = np.stack([wq, wk, np.asarray(i["L0_attn_Wv"]), np.asarray(i["L0_attn_Wo"])], axis=1)
    b_cols = np.concatenate([by_ab_d_pair(np.asarray(i[f"L0_attn_b{n}"])[None]) for n in "qk"]).T
    b_rows = np.concatenate([np.asarray(i["L0_attn_bv"]), np.asarray(i["L0_attn_bo"]), np.asarray(i["L0_ffn_router_bias"])])[None]
    rows = lambda w: np.asarray(w).transpose(1, 0, 2).reshape(P, -1)
    w_ffn = np.concatenate([np.asarray(i["L0_ffn_sw1"]), np.asarray(i["L0_ffn_sw3"]), rows(i["L0_ffn_ew1"]),
                            rows(np.asarray(i["L0_ffn_sw2"]).reshape(NSH, P, P)), rows(i["L0_ffn_ew2"]),
                            np.asarray(i["L0_ffn_router_w"]).T], axis=1)
    return dict(zip(_ARGS, (np.asarray(i["L0_attn_x"]), w_attn, b_cols, b_rows, w_ffn)))


def kernel(**inputs):
    import concourse.bacc as _bacc
    from concourse.bass_utils import run_bass_kernel_spmd as _run

    nc = _bacc.Bacc("TRN2", target_bir_lowering=False, num_devices=1)
    arrays = {f"{n}_dram": np.ascontiguousarray(a) for n, a in lay_out(inputs).items()}
    args = [nc.dram_tensor(n, a.shape, mybir.dt.from_np(a.dtype), kind="ExternalInput").ap() for n, a in arrays.items()]
    args.append(nc.dram_tensor("out_dram", (NB, S, P), F32, kind="ExternalOutput").ap())
    build_layer(nc, *args)
    return _run(nc, [arrays], core_ids=[0]).results[0]["out_dram"]
```

```python
from contextlib import ExitStack

import numpy as np

import concourse.bass as bass
from concourse import mybir

F32 = mybir.dt.float32
F32R = mybir.dt.float32r
ALU = mybir.AluOpType
ACT = mybir.ActivationFunctionType
AX = mybir.AxisListType

P = 128
NB, S = 8, 256
H, HD = 16, 8
TOK = NB * S
NTILE = TOK // P
GT = 512
NG = TOK // GT
TPG = GT // P
QT = S // P
NAB, NPAIR = 2, 8
HPS = 4
SPB = H // HPS
NSTEP = NB * SPB
NRING = 2
NMAX = 3
LEAD = 6
NSLOT = 4
NE = 8
PIECES = 16
NSH = 2
VW = HD + 1
ROW0 = HD * NAB
ZERO_ROW = 96
SCALE = float(np.float32(1.0) / np.sqrt(np.float32(HD)))
EPS = 1e-5
W1, W3, E1, W2, E2, RW = 0, 256, 512, 512 + NE * P, 512 + NE * P + 256, 512 + 2 * NE * P + 256
WCOLS = RW + NE


def build_layer(nc, x, w_attn, b_rows, w_ffn, out):
    ctx = ExitStack()
    with ctx:
        def sb(name, shape, dt=F32):
            return ctx.enter_context(nc.sbuf_tensor(name, shape, dt))

        def sem(name):
            return ctx.enter_context(nc.semaphore(name))

        gate_dram = nc.dram_tensor("gate_scratch", (NE, TOK), F32, kind="Internal").ap()

        wa_all = sb("wa", [P, 4 * P + 3])
        wa = wa_all[:, 0:4 * P].rearrange("p (w d) -> p w d", w=4)
        bqkv = wa_all[:, 4 * P:]
        brow = sb("brow", [P, P + NE])
        bo_all = sb("bo_all", [P, P])
        wf = sb("wf", [P, RW])
        rw = sb("rw", [P, NE])
        wf_hi = sb("wf_hi", [P, RW], F32R)
        rw_parts = sb("rw_parts", [P, 2, NE], F32R)
        ident = sb("ident", [P, P])
        earlier = sb("earlier", [P, NE, NE])
        minus_half = sb("minus_half", [P, TPG])
        zero_col = sb("zero_col", [P, 1])
        one_rows = sb("one_rows", [2, 1, S], F32R)

        xs = sb("xs", [P, NTILE, P])
        yt_hi = sb("yt_hi", [P, TOK], F32R)
        yt_lo = sb("yt_lo", [P, TOK], F32R)

        qk_parts = sb("qk_parts", [P, 2, 4 * GT], F32R)
        parts = [m.rearrange("p (i h t) -> p i h t", i=2, h=2) for m in
                 (qk_parts[:, 0, :], qk_parts[:, 1, :], wf_hi[:, 0:4 * GT], wf[:, 0:4 * GT].bitcast(F32R))]
        wf_lo = qk_parts[:, :, :].rearrange("p g t -> p (g t)")[:, 0:RW]
        qstack = sb("qstack", [P, NSLOT, NPAIR, S], F32R)
        kstack = sb("kstack", [P, NSLOT, NAB, NPAIR, S], F32R)
        v = sb("v", [P, NTILE * H // 2, 3 * VW])
        v_parts = v[:, :, :].rearrange("p n (k w) -> p n k w", k=3)
        top = sb("top", [P, QT, H])
        top_parts = sb("top_parts", [P, 2, QT, NAB, 2, NPAIR], F32R)
        top_rows = sb("top_rows", [NAB * 2 * NPAIR, 2, S], F32R)
        probs_mem = sb("probs_mem", [P, 4 * HPS * S])
        probs = probs_mem[:, :].rearrange("p (n j q) -> p n (j q)", n=4, j=HPS)
        xt = probs_mem[:, 0:NG * GT].rearrange("p (g t) -> p g t", t=GT)
        qk = probs_mem[:, NG * GT:].rearrange("p (g i t) -> p g i t", g=2, i=2)
        att_raw = sb("att_raw", [P, 2, SPB // 2, S])
        rsum = sb("rsum", [P, QT * H // 2, 2])
        att = sb("att", [P, QT, P])
        att_t = sb("att_t", [P, S])
        res1 = sb("res1", [P, QT, P])
        stats1 = sb("stats1", [P, QT, 6])
        mv1 = sb("mv1", [P, QT, 2])
        rstd1 = sb("rstd1", [P, QT])

        expl = sb("expl", [P, TPG, NE])
        sig = sb("sig", [P, TPG, NE])
        sel = sb("sel", [P, TPG, NE])
        diff = sb("diff", [P, TPG, NE, NE])
        tie = sb("tie", [P, TPG, NE, NE])
        rank = sb("rank", [P, TPG, NE])
        mask = sb("mask", [P, TPG, NE])
        picked = sb("picked", [P, TPG, NE])
        den = sb("den", [P, TPG])
        den_ok = sb("den_ok", [P, TPG])
        den_inv = sb("den_inv", [P, TPG])
        equal_share = sb("equal_share", [P, TPG])
        comb = sb("comb", [P, TPG, NE])
        comb_t = sb("comb_t", [NE, 2, S])

        sh_hi = kstack[:, 0, :, :, :].rearrange("p a r q -> p (a r q)").rearrange("p (j t) -> p j t", j=NSH)
        sh_lo = kstack[:, 1, :, :, :].rearrange("p a r q -> p (a r q)").rearrange("p (j t) -> p j t", j=NSH)
        gates = [kstack[:, 2 + i, :, :, :].rearrange("p a r q -> p (a r q)").rearrange("p (e t) -> p e t", e=NE).bitcast(F32)
                 for i in range(2)]
        hid_hi = qstack[:, 0, :, :].rearrange("p r q -> p (r q)").rearrange("p (n t) -> p n t", n=4)
        hid_lo = qstack[:, 1, :, :].rearrange("p r q -> p (r q)").rearrange("p (n t) -> p n t", n=4)
        ffn = probs_mem[:, :].rearrange("p (n t) -> p n t", n=8)
        act_out, hid, acc_t = ffn[:, 0:2, :], ffn[:, 2:4, :], ffn[:, 4, :]
        res2 = ffn[:, 5, :].rearrange("p (t d) -> p t d", t=TPG)
        stats2 = ffn[:, 6, 0:6 * TPG].rearrange("p (t n) -> p t n", t=TPG)
        mv2 = ffn[:, 6, 64:64 + 2 * TPG].rearrange("p (t n) -> p t n", t=TPG)
        rstd2 = ffn[:, 6, 128:128 + TPG]

        ring = [ctx.enter_context(nc.psum_tensor(f"ring{i}", [P, 512], F32)) for i in range(NRING)]
        max_bank = [ctx.enter_context(nc.psum_tensor(f"max_bank{i}", [P, 512], F32)) for i in range(NMAX)]
        pv_bank = ctx.enter_context(nc.psum_tensor("pv_bank", [P, 512], F32))
        misc_bank = [ctx.enter_context(nc.psum_tensor(f"misc_bank{i}", [P, 512], F32)) for i in range(2)]
        pro_bank = ring + misc_bank
        shared_bank = [max_bank[0:2], ring[0:2]]
        expert_bank = [max_bank[2]] + ring

        x_loaded = [sem(f"x_loaded{g}") for g in range(NG)]
        wa_loaded, brow_loaded, rw_loaded, wf_loaded = (
            sem("wa_loaded"), sem("brow_loaded"), sem("rw_loaded"), sem("wf_loaded"))
        ident_set, rows_set, zero_set, earlier_set = sem("ident_set"), sem("rows_set"), sem("zero_set"), sem("earlier_set")
        v_ones_set, pv_cleared = sem("v_ones_set"), sem("pv_cleared")
        q_cleared = [sem(f"q_cleared{i}") for i in range(NSLOT)]
        k_cleared = [sem(f"k_cleared{i}") for i in range(NSLOT)]
        pro_made, pro_act, pro_dve = sem("pro_made"), sem("pro_act"), sem("pro_dve")
        qk_hi_made, qk_lo_made = sem("qk_hi_made"), sem("qk_lo_made")
        first_q_loaded = sem("first_q_loaded")
        ones_loaded = [sem(f"ones_loaded{i}") for i in range(NSLOT)]
        stack_loaded = [sem(f"stack_loaded{i}") for i in range(NSLOT)]
        shift_loaded = [sem(f"shift_loaded{i}") for i in range(2)]
        max_scores, max_taken, top_split = sem("max_scores"), sem("max_taken"), sem("top_split")
        scores_made, probs_made, pv_made, pv_taken = sem("scores_made"), sem("probs_made"), sem("pv_made"), sem("pv_taken")
        misc_made, misc_act, misc_dve = sem("misc_made"), sem("misc_act"), sem("misc_dve")
        dve_chain, pool_chain = sem("dve_chain"), sem("pool_chain")
        xb_made, stats_made, rstd_made, y_made, yt_hi_made = (
            sem("xb_made"), sem("stats_made"), sem("rstd_made"), sem("y_made"), sem("yt_hi_made"))
        route_dve, route_pool = sem("route_dve"), sem("route_pool")
        gate_stored, gates_loaded = (
            [sem(f"{n}{i}") for i in range(2)] for n in ("gate_stored", "gates_loaded"))
        rw_split, w_hi_made, w_split = sem("rw_split"), sem("w_hi_made"), sem("w_split")
        up_made, act_made, hid_made, hi_made, down_made = (
            sem("up_made"), sem("act_made"), sem("hid_made"), sem("hi_made"), sem("down_made"))
        lo_made = [sem("lo_made_even"), sem("lo_made_odd")]
        acc_taken, fin_made, fin_stats, fin_rstd, fin_out = (
            sem("acc_taken"), sem("fin_made"), sem("fin_stats"), sem("fin_rstd"), sem("fin_out"))
        out_stored = sem("out_stored")

        UP0 = NSTEP
        EX0 = UP0 + NG * NSH
        NEX = NG * NE
        NHID = NG * NSH + NEX
        LAG = 3
        LAST = EX0 + NEX + LAG + 9
        HALVES = [(t, half) for t in range(-LEAD, LAST) for half in range(2)]
        jobs = {h: [] for h in HALVES}

        PRO = [(k, g) for g in range(NG) for k in ("xT", "k", "q", "v")] + [("bo", 0)]
        for g in range(1, NG):
            n = 4 * g
            PRO[n - 1], PRO[n] = PRO[n], PRO[n - 1]
        PRE = 10
        for n in range(PRE, len(PRO)):
            jobs[(n - PRE + 1) // 2 - LEAD, (n - PRE + 1) % 2].append(("project", n))
        for b in range(NB):
            jobs[SPB * b - 2, 0].append(("shift", b))
            first = SPB * (b + 1)
            when = {"norm": 2, "attT": 3, "wo": 4, "y": 5, "yT": 7}
            if b == NB - 1:
                when = {"norm": 1, "attT": 3, "wo": 5, "y": 9, "yT": 11}
            for kind, half_tick in when.items():
                jobs[first + half_tick // 2, half_tick % 2].append((kind, b))
            late = b // 2 == NG - 1
            router = 2 * EX0 if late else 2 * first + (9 if b < 2 else 8)
            jobs[router // 2, router % 2].append(("router", b))
            if b % 2:
                for kind, n in (("route0", 1), ("sig", 2), ("route1", 3), ("route2", 4), ("route3", 6),
                                ("rank", 8), ("route4", 9), ("den", 10), ("route5", 11)):
                    n = router + n * (2 if late else 1)
                    jobs[n // 2, n % 2].append((kind, b // 2))
                comb_tick = {NG - 1: EX0 + 16, NG - 2: EX0 + 1}.get(b // 2, router // 2 + 7)
                for i in range(2):
                    jobs[comb_tick, i].append(("combT", b - 1 + i))
        for g in range(NG):
            jobs[max(UP0 + 1, EX0 + NE * (g - 1)), 1].append(("load gates", g))
        for n in range(NG * NSH):
            jobs[UP0 + n, 1].append(("hidden", n))
        for m in range(NEX):
            jobs[EX0 + m, 0].append(("hidden", NG * NSH + m))
            jobs[EX0 + m + LAG, 1].append(("down", m))
            if m % NE == NE - 1:
                g = m // NE
                for kind, i in (("accT", 0), ("finT", 1), ("rstd2", 2), ("norm2", 7)):
                    jobs[EX0 + m + LAG + 1 + i, 0].append((kind, g))
        jobs[UP0 + NHID, 0].append(("last parts", 0))

        def step(t):
            return 0 <= t < NSTEP

        PRO_TAKER = {(k, g): "dve" if k == "bo" or k in ("q", "k") and g < 2 else "act" for k, g in PRO}
        PRO_READ = {"act": pro_act, "dve": pro_dve}
        pro_taken = {u: sum(PRO_TAKER[w] == PRO_TAKER[u] for w in PRO[:n + 1]) for n, u in enumerate(PRO)}
        hi_order = [u for u in PRO if u[0] in ("q", "k")]

        def wait_pro(eng, u):
            eng.wait_ge(PRO_READ[PRO_TAKER[u]], pro_taken[u])

        def wait_hi(eng, u):
            eng.wait_ge(qk_hi_made, hi_order.index(u) + 1)

        TAKER = {"shift": "act", "norm": "dve",
                 "attT": "act", "wo": "dve", "yT": "dve", "router": "act", "combT": "act"}
        MISC_READ = {"act": misc_act, "dve": misc_dve}
        uses = [u for h in HALVES for u in jobs[h] if u[0] in TAKER]
        made = {u: i + 1 for i, u in enumerate(uses)}
        taken = {u: sum(TAKER[w[0]] == TAKER[u[0]] for w in uses[:i + 1]) for i, u in enumerate(uses)}

        def heads_of(i):
            n, k = divmod(i % SPB, 2)
            return [(n, 2 * j + k) for j in range(HPS)]

        def misc_of(u):
            return misc_bank[made[u] % 2]

        def wait_taken(eng, u):
            eng.wait_ge(MISC_READ[TAKER[u[0]]], taken[u])

        def wait_parts(eng, i, g, lo):
            u = ("qk"[i], g)
            if not lo:
                wait_hi(eng, u)
            elif g < 2:
                wait_pro(eng, u)
            else:
                eng.wait_ge(qk_lo_made, hi_order.index(u) - 3)

        def wait_stack(eng, b):
            s = b % NSLOT
            eng.wait_ge(stack_loaded[s], 16 * (9 * (b // NSLOT + 1) + 2 * (b // NSLOT) - (3 if s == 0 else 0)))
            if b == 0:
                eng.wait_ge(first_q_loaded, 16 * 3)

        def link(eng, chain, count, ins):
            count[0] += 1
            ins.then_inc(chain, 1)
            eng.wait_ge(chain, count[0])

        def hidden_parts(n):
            if n < NG * NSH:
                g, j = divmod(n, NSH)
                return sh_hi[:, j, tokens(g)], sh_lo[:, j, tokens(g)]
            return hid_hi[:, n % 4, :], hid_lo[:, n % 4, :]

        def lo_by_dve(n):
            return n % 2 == 0 or n in (NG * NSH - 1, NG * NSH + 1, NHID - 1)

        def tokens(g):
            return slice(g * GT, (g + 1) * GT)

        def tiles(g):
            return slice(g * TPG, (g + 1) * TPG)

        def stack_q(eng, b):
            g, t0 = b // 2, b % 2 * S
            eng.wait_ge(q_cleared[b % NSLOT], 1)
            for i, part in enumerate((0, 0, 1)):
                wait_parts(eng, 0, g, part)
                r = 32 * i + ROW0
                eng.dma_start(qstack[r:r + NAB * HD, b % NSLOT, :, :].bitcast(F32),
                              parts[g][:, 0, part, t0:t0 + S].bitcast(F32)).then_inc(
                                  stack_loaded[b % NSLOT] if b else first_q_loaded, 16)

        block = ctx.enter_context(nc.Block())

        @block.sync
        def _(sp):
            xg = x.rearrange("b (t p) d -> p (b t) d", p=P)
            outg = out.rearrange("b (t p) d -> p (b t) d", p=P)
            sp.dma_start(xs[:, tiles(0), :], xg[:, tiles(0), :]).then_inc(x_loaded[0], 16)
            for g in range(1, NG):
                sp.dma_start(xs[:, tiles(g), :], xg[:, tiles(g), :]).then_inc(x_loaded[g], 16)
            sp.dma_start(brow[:, :], b_rows.to_broadcast([P, P + NE])).then_inc(brow_loaded, 16)

            def move(dst, src):
                return sp.dma_start(dst.bitcast(F32), src.bitcast(F32))

            def ones(b):
                sp.wait_ge(rows_set, 1)
                sp.wait_ge(k_cleared[b], 1)
                for ab in range(NAB):
                    move(kstack[32 * ab:32 * ab + 2, b, ab, :, :],
                         one_rows[:, :, :].to_broadcast([2, NPAIR, S])).then_inc(ones_loaded[b], 16)

            def stack(b):
                s, g, t0 = b % NSLOT, b // 2, (b % 2) * S
                if b < NSLOT:
                    ones(b)
                else:
                    sp.wait_ge(scores_made, 4 * SPB * (b - NSLOT + 1))
                    for r in (0, 32):
                        move(qstack[r:r + 2, s, :, :], kstack[ZERO_ROW:ZERO_ROW + 2, s, 0, :, :]).then_inc(stack_loaded[s], 16)
                for i, part in ((0, 0), (2, 0), (1, 1)):
                    wait_parts(sp, 1, g, part)
                    for ab in range(NAB):
                        r = 32 * i + ROW0 + HD * ab
                        move(kstack[r:r + HD, s, ab, :, :],
                             parts[g][64 * ab:64 * ab + 64, 1, part, t0:t0 + S]).then_inc(stack_loaded[s], 16)
                if b:
                    stack_q(sp, b)

            def load_gates(g):
                if g < 2:
                    sp.wait_ge(scores_made, 4 * NSTEP)
                else:
                    sp.wait_ge(hid_made, NG * NSH + NE * (g - 1))
                for i in range(2):
                    sp.wait_ge(gate_stored[i], 16 * (g + 1))
                src = gate_dram.rearrange("(o e) t -> o e t", o=1)[:, :, tokens(g)]
                sp.dma_start(gates[g % 2], src.to_broadcast([P, NE, GT])).then_inc(gates_loaded[g % 2], 16)

            for b in range(3):
                stack(b)
            for tick, half in HALVES:
                for kind, b in jobs[tick, half]:
                    if kind == "shift":
                        wait_taken(sp, (kind, b))
                        for ab in range(NAB):
                            move(qstack[32 * ab:32 * ab + 2, b % NSLOT, :, :],
                                 top_rows[16 * ab:16 * ab + 16, b % 2, :]).then_inc(shift_loaded[b % 2], 16)
                        if b == 0:
                            stack(3)
                    if kind == "combT":
                        wait_taken(sp, (kind, b))
                        sp.dma_start(gate_dram[:, b * S:(b + 1) * S], comb_t[:, b % 2, :]).then_inc(gate_stored[b % 2], 16)
                    if kind == "norm2":
                        sp.wait_ge(fin_out, b + 1)
                        sp.dma_start(outg[:, tiles(b), :], xs[:, tiles(b), :]).then_inc(out_stored, 16)
                    if kind == "load gates":
                        load_gates(b)
                if half and step(tick) and tick % SPB == 3 and tick // SPB + NSLOT < NB:
                    stack(tick // SPB + NSLOT)
                    if tick // SPB + NSLOT == NB - 1:
                        for b in (NB - 2, NB - 1):
                            wait_stack(sp, b)
                        sp.dma_start(wf[:, :], w_ffn[:, 0:RW]).then_inc(wf_loaded, 16)
            sp.wait_ge(out_stored, 16 * NG)

        @block.gpsimd
        def _(pool):
            cnt = [0]

            def chain(ins):
                link(pool, pool_chain, cnt, ins)

            chain(pool.memset(ident[:, :], 0.0))
            pool.affine_select(out=ident[:, :], in_=ident[:, :], compare_op=ALU.not_equal, fill=1.0, base=0,
                               pattern=[[-1, P]], channel_multiplier=1).then_inc(ident_set, 1)
            pool.memset(one_rows[:, :, :].bitcast(F32), 1.0).then_inc(rows_set, 1)
            def clear(s):
                pool.memset(kstack[:, s, :, :, :].bitcast(F32), 0.0).then_inc(k_cleared[s], 1)
                pool.memset(qstack[:, s, :, :].bitcast(F32), 0.0).then_inc(q_cleared[s], 1)

            clear(2)
            stack_q(pool, 0)
            pool.memset(v_parts[:, :, 0:3:2, HD:VW], 1.0).then_inc(v_ones_set, 1)
            pool.memset(v_parts[:, :, 1, :], 0.0).then_inc(v_ones_set, 1)
            clear(3)
            pool.memset(minus_half[:, :], -0.5)
            chain(pool.memset(earlier[:, :, :], 1.0))
            pool.affine_select(out=earlier[:, :, :], in_=earlier[:, :, :], compare_op=ALU.is_gt, fill=0.0, base=0,
                               pattern=[[1, NE], [-1, NE]], channel_multiplier=0).then_inc(earlier_set, 1)
            pool.wait_ge(rw_loaded, 16)
            chain(pool.tensor_scalar(rw_parts[:, 0, :], rw[:, :], 1.0, None, ALU.mult))
            pool.tensor_tensor(rw_parts[:, 1, :], rw[:, :], rw_parts[:, 0, :].bitcast(F32), ALU.subtract).then_inc(rw_split, 1)
            for n, (kind, g) in enumerate(hi_order[4:]):
                i = "qk".index(kind)
                pool.wait_ge(qk_hi_made, n + 5)
                wait_pro(pool, (kind, g))
                pool.tensor_tensor(parts[g][:, i, 1, :], qk[:, g - 2, i, :], parts[g][:, i, 0, :].bitcast(F32),
                                   ALU.subtract).then_inc(qk_lo_made, 1)
            wait_pro(pool, ("bo", 0))
            for g in range(NG):
                pool.tensor_tensor(xs[:, tiles(g), :], xs[:, tiles(g), :],
                                   bo_all[:, None, :].to_broadcast([P, TPG, P]), ALU.add).then_inc(xb_made, 1)
            cuts = [slice(c, c + RW // PIECES) for c in range(0, RW, RW // PIECES)]
            assert cuts[-1].stop == RW

            for tick, half in HALVES:
                piece = 2 * (tick - SPB * (NSLOT + 1)) + half
                if 0 <= piece < PIECES:
                    if piece == 0:
                        pool.wait_ge(wf_loaded, 16)
                        for b in range(NSLOT, NB):
                            wait_stack(pool, b)
                    c = cuts[piece]
                    pool.tensor_scalar(wf_hi[:, c], wf[:, c], 1.0, None, ALU.mult).then_inc(w_hi_made, 1)
                    pool.wait_ge(w_hi_made, piece + 1)
                    pool.tensor_tensor(wf_lo[:, c], wf[:, c], wf_hi[:, c].bitcast(F32), ALU.subtract).then_inc(w_split, 1)
                for kind, n in jobs[tick, half]:
                    if kind == "wo":
                        pool.wait_ge(stats_made, n + 1)
                        chain(pool.tensor_scalar(rstd1[:, :], mv1[:, :, 1], EPS, None, ALU.add))
                        pool.tensor_tensor(rstd1[:, :], rstd1[:, :], minus_half[:, 0:QT], ALU.pow).then_inc(rstd_made, 1)
                    if kind == "rstd2":
                        pool.wait_ge(fin_stats, n + 1)
                        chain(pool.tensor_scalar(rstd2, mv2[:, :, 1], EPS, None, ALU.add))
                        pool.tensor_tensor(rstd2, rstd2, minus_half[:, :], ALU.pow).then_inc(fin_rstd, 1)
                    if kind == "route0":
                        wait_taken(pool, ("router", 2 * n + 1))
                        pool.tensor_scalar(expl[:, :, :], expl[:, :, :], 1.0, None, ALU.add).then_inc(route_pool, 1)
                    if kind == "route1":
                        pool.wait_ge(route_dve, 3 * n + 1)
                        chain(pool.tensor_tensor(sel[:, :, :], sig[:, :, :],
                                                 brow[:, None, P:].to_broadcast([P, TPG, NE]), ALU.add))
                        for t in range(TPG):
                            ins = pool.tensor_tensor(diff[:, t, :, :], sel[:, t, None, :].to_broadcast([P, NE, NE]),
                                                     sel[:, t, :, None].to_broadcast([P, NE, NE]), ALU.subtract)
                        chain(ins)
                    if kind == "route2":
                        if n == 0:
                            pool.wait_ge(earlier_set, 1)
                        pool.tensor_scalar(tie[:, :, :, :], diff[:, :, :, :], 0.0, None, ALU.is_equal)
                        chain(pool.tensor_scalar(diff[:, :, :, :], diff[:, :, :, :], 0.0, None, ALU.is_gt))
                    if kind == "route3":
                        for t in range(TPG):
                            ins = pool.tensor_tensor(tie[:, t, :, :], tie[:, t, :, :], earlier[:, :, :], ALU.mult)
                        chain(ins)
                        pool.tensor_tensor(diff[:, :, :, :], diff[:, :, :, :], tie[:, :, :, :],
                                           ALU.add).then_inc(route_pool, 1)
                    if kind == "route4":
                        pool.wait_ge(route_dve, 3 * n + 2)
                        chain(pool.tensor_scalar(mask[:, :, :], rank[:, :, :], 1.5, None, ALU.is_lt))
                        pool.tensor_tensor(picked[:, :, :], mask[:, :, :], sig[:, :, :], ALU.mult).then_inc(route_pool, 1)
                    if kind == "route5":
                        pool.wait_ge(route_dve, 3 * n + 3)
                        chain(pool.tensor_scalar(den_ok[:, :], den[:, :], 1e-9, None, ALU.is_gt))
                        chain(pool.tensor_scalar(equal_share[:, :], den_ok[:, :], -0.5, 0.5, ALU.mult, ALU.add))
                        chain(pool.tensor_tensor(den_inv[:, :], den_inv[:, :], den_ok[:, :], ALU.mult))
                        chain(pool.tensor_tensor(picked[:, :, :], picked[:, :, :],
                                                 den_inv[:, :, None].to_broadcast([P, TPG, NE]), ALU.mult))
                        chain(pool.tensor_tensor(mask[:, :, :], mask[:, :, :],
                                                 equal_share[:, :, None].to_broadcast([P, TPG, NE]), ALU.mult))
                        if n:
                            pool.wait_ge(misc_made, made["combT", 2 * n - 1])
                        pool.tensor_tensor(comb[:, :, :], picked[:, :, :], mask[:, :, :], ALU.add).then_inc(route_pool, 1)
                    if kind == "hidden" and not lo_by_dve(n):
                        pool.wait_ge(hi_made, n + 1)
                        hi, lo = hidden_parts(n)
                        pool.tensor_tensor(lo, hid[:, 1, :], hi.bitcast(F32), ALU.subtract).then_inc(lo_made[1], 1)
        @block.scalar
        def _(act):
            act.dma_start(wa_all[:, :], w_attn).then_inc(wa_loaded, 16)

            act.dma_start(rw[:, :], w_ffn[:, RW:]).then_inc(rw_loaded, 16)
            def take_projection(n):
                kind, g = PRO[n]
                bank = pro_bank[n % len(pro_bank)]
                if kind == "bo":
                    return
                act.wait_ge(pro_made, n + 1)
                if kind == "xT":
                    nc.scalar.copy(xt[:, g, :], bank[:, :]).then_inc(pro_act, 1)
                elif kind == "v":
                    nc.scalar.copy(v_parts[:, g * TPG * H // 2:(g + 1) * TPG * H // 2, 0:3:2, 0:HD],
                                   bank[:, :].rearrange("p (n k d) -> p n k d", k=2, d=HD)).then_inc(pro_act, 1)
                else:
                    i = "qk".index(kind)
                    if n == 1:
                        act.wait_ge(wa_loaded, 16)
                    nc.scalar.activation(parts[g][:, i, 0, :], bank[:, :], ACT.Identity,
                                         bias=bqkv[:, i:i + 1]).then_inc(qk_hi_made, 1)
                    if g >= 2:
                        nc.scalar.activation(qk[:, g - 2, i, :], bank[:, :], ACT.Identity,
                                             bias=bqkv[:, i:i + 1]).then_inc(pro_act, 1)

            def hi_part(n):
                m = n - NG * NSH
                act.wait_ge(hid_made, n + 1)
                if m >= 4:
                    act.wait_ge(down_made, m - 3)
                nc.scalar.copy(hidden_parts(n)[0], hid[:, n % 2, :]).then_inc(hi_made, 1)

            for n in range(PRE):
                take_projection(n)
            for tick, half in HALVES:
                for c in (2 * half, 2 * half + 1):
                    if step(tick):
                        k = 4 * tick + c
                        act.wait_ge(scores_made, k + 1)
                        if tick >= 2:
                            act.wait_ge(pv_made, tick - 1)
                        if k == 4:
                            act.wait_ge(qk_lo_made, 4)
                        nc.scalar.activation(probs[:, k // 2 % 4, c % 2 * 512:(c % 2 + 1) * 512], ring[k % NRING][:, :],
                                             ACT.Exp, scale=SCALE).then_inc(probs_made, 1)
                    if c == 2 and step(tick - 1) and tick % 2 == 0:
                        i = tick - 1
                        act.wait_ge(pv_made, i + 1)
                        nc.scalar.copy(att_raw[:, i // SPB % 2, i % SPB // 2, :], pv_bank[:, 0:S]).then_inc(pv_taken, 1)
                for kind, b in jobs[tick, half]:
                    if TAKER.get(kind) == "act" or kind == "yT":
                        act.wait_ge(misc_made, made[kind, b])
                    if kind == "project":
                        take_projection(b)
                    if kind in TAKER:
                        misc = misc_of((kind, b))
                    if kind == "shift":
                        if b >= 2:
                            act.wait_ge(shift_loaded[b % 2], 32 * (b // 2))
                        nc.scalar.copy(top_rows[:, b % 2, :], misc[0:NAB * 2 * NPAIR, 0:S]).then_inc(misc_act, 1)
                    if kind == "attT":
                        nc.scalar.copy(att_t[:, :], misc[:, 0:S]).then_inc(misc_act, 1)
                    if kind == "yT":
                        nc.scalar.copy(yt_hi[:, b * S:(b + 1) * S], misc[:, 0:S]).then_inc(yt_hi_made, 1)
                    if kind == "router":
                        if b % 2 == 0 and b:
                            act.wait_ge(route_dve, 3 * (b // 2) - 2)
                        nc.scalar.activation(expl[:, QT * (b % 2):QT * (b % 2) + QT, :],
                                             misc[:, 0:QT * NE].rearrange("p (t e) -> p t e", e=NE), ACT.Exp,
                                             scale=-1.0).then_inc(misc_act, 1)
                    if kind == "combT":
                        if b >= 2:
                            act.wait_ge(gate_stored[b % 2], 16 * (b // 2))
                        nc.scalar.copy(comb_t[:, b % 2, :], misc[0:NE, 0:S]).then_inc(misc_act, 1)
                    if kind == "hidden":
                        act.wait_ge(up_made, b + 1)
                        if b >= 2:
                            act.wait_ge(hid_made, b - 1)
                        if b < NG * NSH:
                            nc.scalar.activation(act_out[:, b % 2, :], shared_bank[b % 2][0][:, :], ACT.Silu).then_inc(act_made, 1)
                        else:
                            nc.scalar.activation(act_out[:, b % 2, :], expert_bank[(b - NG * NSH) % 3][:, :], ACT.Gelu).then_inc(act_made, 1)
                        if b:
                            hi_part(b - 1)
                    if kind == "last parts":
                        hi_part(NHID - 1)
                    if kind == "accT":
                        act.wait_ge(down_made, NE * (b + 1))
                        if b:
                            act.wait_ge(fin_made, b)
                        nc.scalar.copy(acc_t, max_bank[b % 2][:, :]).then_inc(acc_taken, 1)

        @block.vector
        def _(dve):
            cnt = [0]

            def chain(ins):
                link(dve, dve_chain, cnt, ins)

            dve.memset(zero_col[:, :], 0.0).then_inc(zero_set, 1)
            dve.wait_ge(zero_set, 1)

            def clear(tile, n, cleared):
                dve.tensor_copy(tile, zero_col[:, :].to_broadcast([P, n])).then_inc(cleared, 1)

            def take_projection(n):
                kind, g = PRO[n]
                bank = pro_bank[n % len(pro_bank)]
                if kind in ("q", "k") and g < 2:
                    i = "qk".index(kind)
                    wait_hi(dve, (kind, g))
                    dve.scalar_tensor_tensor(out=parts[g][:, i, 1, :], in0=bank[:, :], scalar=bqkv[:, i:i + 1],
                                             in1=parts[g][:, i, 0, :].bitcast(F32), op0=ALU.add,
                                             op1=ALU.subtract).then_inc(pro_dve, 1)
                if kind == "bo":
                    dve.wait_ge(brow_loaded, 16)
                    dve.wait_ge(pro_made, n + 1)
                    dve.tensor_tensor(bo_all[:, :], bank[:, 0:P], brow[:, 0:P], ALU.add).then_inc(pro_dve, 1)

            for s in range(2):
                clear(kstack[:, s, :, :, :].rearrange("p a r q -> p (a r q)"), NAB * NPAIR * S, k_cleared[s])
                clear(qstack[:, s, :, :].rearrange("p r q -> p (r q)"), NPAIR * S, q_cleared[s])
            dve.memset(pv_bank[:, :], 0.0).then_inc(pv_cleared, 1)
            def lo_part(n):
                dve.wait_ge(hi_made, n + 1)
                hi, lo = hidden_parts(n)
                dve.tensor_tensor(lo, hid[:, n % 2, :], hi.bitcast(F32), ALU.subtract).then_inc(lo_made[n % 2], 1)

            dve.wait_ge(wa_loaded, 16)
            for n in range(PRE):
                take_projection(n)
            for tick, half in HALVES:
                if step(tick + LEAD):
                    i = tick + LEAD
                    b, heads = i // SPB, heads_of(i)
                    if i % SPB == 0 and b and not half:
                        dve.wait_ge(top_split, b)
                    for c in range(2):
                        ab, r = heads[2 * c]
                        h, n = ab * NPAIR + r, 4 * i + 2 * half + c
                        dve.wait_ge(max_scores, n + 1)
                        dve.tensor_reduce(top[:, half, h:h + 3:2], max_bank[n % NMAX][:, :].rearrange("p (h k) -> p h k", h=2),
                                          AX.X, ALU.max).then_inc(max_taken, 1)
                    if half and i % SPB == SPB - 1:
                        dve.wait_ge(max_taken, 4 * (i + 1))
                        if b >= 2:
                            dve.wait_ge(misc_made, made["shift", b - 2])
                        tops = top[:, :, :].rearrange("p q (a r) -> p q a r", a=NAB)
                        hi, lo = (top_parts[:, b % 2, :, :, n, :] for n in range(2))
                        chain(dve.tensor_scalar(hi, tops, -1.0, None, ALU.mult))
                        dve.scalar_tensor_tensor(out=lo, in0=tops, scalar=-1.0, in1=hi.bitcast(F32), op0=ALU.mult,
                                                 op1=ALU.subtract).then_inc(top_split, 1)
                for kind, b in jobs[tick, half]:
                    if kind in TAKER:
                        misc = misc_of((kind, b))
                    if kind == "project":
                        take_projection(b)
                    if kind == "norm":
                        dve.wait_ge(misc_made, made[kind, b])
                        heads = misc[:, :].rearrange("p (n r) -> p n r", r=32)[:, :, 0:2 * VW].rearrange(
                            "p n (k w) -> p n k w", k=2)
                        chain(dve.reciprocal(rsum[:, :, :], heads[:, :, :, HD]))
                        dve.tensor_tensor(att[:, :, :].rearrange("p t (n k d) -> p (t n) k d", k=2, d=HD), heads[:, :, :, 0:HD],
                                          rsum[:, :, :, None].to_broadcast([P, QT * H // 2, 2, HD]),
                                          ALU.mult).then_inc(misc_dve, 1)
                    if kind == "wo":
                        dve.wait_ge(misc_made, made[kind, b])
                        dve.wait_ge(xb_made, b // 2 + 1)
                        if b:
                            dve.wait_ge(y_made, b)
                        dve.tensor_tensor(res1[:, :, :], misc[:, 0:S].rearrange("p (t d) -> p t d", t=QT),
                                          xs[:, QT * b:QT * b + QT, :], ALU.add).then_inc(misc_dve, 1)
                        wait_taken(dve, (kind, b))
                        for t in range(QT):
                            ins = dve.bn_stats(stats1[:, t, :], res1[:, t, :])
                        chain(ins)
                        for t in range(QT):
                            ins = dve.bn_aggr(mv1[:, t, :], stats1[:, t, :])
                        ins.then_inc(stats_made, 1)
                    if kind == "y":
                        dve.wait_ge(rstd_made, b + 1)
                        for t in range(QT):
                            ins = dve.tensor_scalar(xs[:, QT * b + t, :], res1[:, t, :], mv1[:, t, 0:1],
                                                    rstd1[:, t:t + 1], ALU.subtract, ALU.mult)
                        ins.then_inc(y_made, 1)
                    if kind == "yT":
                        dve.wait_ge(yt_hi_made, b + 1)
                        dve.tensor_tensor(yt_lo[:, b * S:(b + 1) * S], misc[:, 0:S],
                                          yt_hi[:, b * S:(b + 1) * S].bitcast(F32), ALU.subtract).then_inc(misc_dve, 1)
                    if kind == "sig":
                        dve.wait_ge(route_pool, 4 * b + 1)
                        dve.reciprocal(sig[:, :, :], expl[:, :, :]).then_inc(route_dve, 1)
                    if kind == "rank":
                        dve.wait_ge(route_pool, 4 * b + 2)
                        dve.tensor_reduce(rank[:, :, :], diff[:, :, :, :], AX.X, ALU.add).then_inc(route_dve, 1)
                    if kind == "den":
                        dve.wait_ge(route_pool, 4 * b + 3)
                        chain(dve.tensor_reduce(den[:, :], picked[:, :, :], AX.X, ALU.add))
                        chain(dve.tensor_scalar(den_inv[:, :], den[:, :], 1e-9, None, ALU.add))
                        dve.reciprocal(den_inv[:, :], den_inv[:, :]).then_inc(route_dve, 1)
                    if kind == "hidden":
                        dve.wait_ge(act_made, b + 1)
                        if b >= 2:
                            dve.wait_ge(lo_made[b % 2], b // 2)
                        m = b - NG * NSH
                        if m >= 0:
                            dve.wait_ge(gates_loaded[m // NE % 2], 16 * (m // NE // 2 + 1))
                        other = shared_bank[b % 2][1][:, :] if m < 0 else gates[m // NE % 2][:, m % NE, :]
                        dve.tensor_tensor(hid[:, b % 2, :], act_out[:, b % 2, :], other, ALU.mult).then_inc(hid_made, 1)
                        if b and lo_by_dve(b - 1):
                            lo_part(b - 1)
                    if kind == "last parts":
                        lo_part(NHID - 1)
                    if kind == "finT":
                        dve.wait_ge(fin_made, b + 1)
                        if b:
                            dve.wait_ge(fin_out, b)
                        chain(dve.tensor_tensor(res2, pv_bank[:, :].rearrange("p (t d) -> p t d", t=TPG),
                                                xs[:, tiles(b), :], ALU.add))
                        for t in range(TPG):
                            ins = dve.bn_stats(stats2[:, t, :], res2[:, t, :])
                        chain(ins)
                        for t in range(TPG):
                            ins = dve.bn_aggr(mv2[:, t, :], stats2[:, t, :])
                        ins.then_inc(fin_stats, 1)
                    if kind == "norm2":
                        dve.wait_ge(fin_rstd, b + 1)
                        for t in range(TPG):
                            ins = dve.tensor_scalar(xs[:, b * TPG + t, :], res2[:, t, :], mv2[:, t, 0:1],
                                                    rstd2[:, t:t + 1], ALU.subtract, ALU.mult)
                        ins.then_inc(fin_out, 1)

        @block.tensor
        def _(pe):
            mm = nc.tensor.matmul

            def project(n):
                kind, g = PRO[n]
                bank = pro_bank[n % len(pro_bank)]
                if n >= len(pro_bank):
                    wait_pro(pe, PRO[n - len(pro_bank)])
                if kind == "xT":
                    pe.wait_ge(x_loaded[g], 16)
                    for t in range(TPG):
                        ins = nc.tensor.transpose(bank[:, t * P:(t + 1) * P], xs[:, g * TPG + t, :], ident[:, :])
                if kind == "k":
                    wait_pro(pe, ("xT", g))
                    pe.wait_ge(wa_loaded, 16)
                if kind in ("q", "k"):
                    ins = mm(bank[:, :], wa[:, "qk".index(kind), :], xt[:, g, :], start=True, stop=True)
                if kind == "v":
                    for t in range(TPG):
                        ins = mm(bank[:, t * P:(t + 1) * P], xt[:, g, t * P:(t + 1) * P], wa[:, 2, :], start=True, stop=True)
                if kind == "bo":
                    ins = mm(bank[:, 0:P], bqkv[:, 2:3].to_broadcast([P, P]), wa[:, 3, :], start=True, stop=True)
                ins.then_inc(pro_made, 1)

            def three(out_ap, w_hi, w_lo, m_hi, m_lo, first, last):
                mm(out_ap, w_lo, m_hi, start=first, stop=False)
                mm(out_ap, w_hi, m_lo, start=False, stop=False)
                return mm(out_ap, w_hi, m_hi, start=False, stop=last)

            def maxima(i, c):
                b, heads = i // SPB, heads_of(i)
                s = b % NSLOT
                if i % SPB == 0 and c == 0:
                    wait_stack(pe, b)
                    pe.wait_ge(ones_loaded[s], 32)
                qt, n = c // 2, 4 * i + c
                if n >= NMAX:
                    pe.wait_ge(max_taken, n - NMAX + 1)
                for j in range(2):
                    ab, r = heads[2 * (c % 2) + j]
                    ins = mm(max_bank[n % NMAX][:, j * S:(j + 1) * S], qstack[:, s, r, qt * P:(qt + 1) * P],
                             kstack[:, s, ab, r, :], start=True, stop=True)
                ins.then_inc(max_scores, 1)

            def scores(i, c):
                b, heads = i // SPB, heads_of(i)
                s, k, kt = b % NSLOT, 4 * i + c, c // 2
                if i % SPB == 0 and c == 0:
                    pe.wait_ge(shift_loaded[b % 2], 32 * (b // 2 + 1))
                if k >= NRING:
                    pe.wait_ge(probs_made, k - NRING + 1)
                for j in range(2):
                    ab, r = heads[2 * (c % 2) + j]
                    ins = mm(ring[k % NRING][:, j * S:(j + 1) * S], kstack[:, s, ab, r, kt * P:(kt + 1) * P],
                             qstack[:, s, r, :], start=True, stop=True)
                ins.then_inc(scores_made, 1)

            def times_v(i, kt):
                b, (n, k) = i // SPB, divmod(i % SPB, 2)
                if kt == 0 and i == 0:
                    pe.wait_ge(v_ones_set, 2)
                    pe.wait_ge(pv_cleared, 1)
                if kt == 0 and k == 0 and i:
                    pe.wait_ge(pv_taken, i // 2)
                pe.wait_ge(probs_made, 4 * i + 2 * kt + 2)
                for j in range(HPS):
                    ins = mm(pv_bank[32 * j:32 * j + 2 * VW, 0:S],
                             v[:, (QT * b + kt) * H // 2 + HPS * n + j, k * VW:(k + 2) * VW],
                             probs[:, (2 * i + kt) % 4, j * S:(j + 1) * S],
                             start=(k == 0 and kt == 0), stop=(k == 1 and kt == QT - 1))
                if kt == QT - 1:
                    ins.then_inc(pv_made, 1)

            pe.wait_ge(ident_set, 1)
            for n in range(PRE):
                project(n)
            for tick, half in HALVES:
                for c in (2 * half, 2 * half + 1):
                    if step(tick):
                        scores(tick, c)
                    if step(tick + LEAD):
                        maxima(tick + LEAD, c)
                    if step(tick - 1) and c % 2 == 0:
                        times_v(tick - 1, half)
                for kind, b in jobs[tick, half]:
                    if kind in TAKER:
                        misc = misc_of((kind, b))
                        if made[kind, b] > 2:
                            wait_taken(pe, uses[made[kind, b] - 3])
                    if kind == "project":
                        project(b)
                    if kind == "shift":
                        if b == 0:
                            wait_pro(pe, ("v", NG - 1))
                            wait_pro(pe, ("bo", 0))
                        pe.wait_ge(top_split, b + 1)
                        for t in range(QT):
                            ins = nc.tensor.transpose(
                                misc[0:NAB * 2 * NPAIR, t * P:(t + 1) * P],
                                top_parts[:, b % 2, t, :, :, :].rearrange("p a n r -> p (a n r)").bitcast(F32), ident[:, :])
                        ins.then_inc(misc_made, 1)
                    if kind == "norm":
                        pe.wait_ge(pv_taken, SPB // 2 * (b + 1))
                        for t in range(QT):
                            for n in range(SPB // 2):
                                ins = nc.tensor.transpose(misc[:, (2 * t + n) * P:(2 * t + n + 1) * P],
                                                          att_raw[:, b % 2, n, t * P:(t + 1) * P], ident[:, :])
                        ins.then_inc(misc_made, 1)
                    if kind == "attT":
                        wait_taken(pe, ("norm", b))
                        for t in range(QT):
                            ins = nc.tensor.transpose(misc[:, t * P:(t + 1) * P], att[:, t, :], ident[:, :])
                        ins.then_inc(misc_made, 1)
                    if kind == "wo":
                        wait_taken(pe, ("attT", b))
                        for t in range(QT):
                            ins = mm(misc[:, t * P:(t + 1) * P], att_t[:, t * P:(t + 1) * P], wa[:, 3, :],
                                     start=True, stop=True)
                        ins.then_inc(misc_made, 1)
                    if kind == "yT":
                        pe.wait_ge(y_made, b + 1)
                        for t in range(QT):
                            ins = nc.tensor.transpose(misc[:, t * P:(t + 1) * P], xs[:, QT * b + t, :], ident[:, :])
                        ins.then_inc(misc_made, 1)
                    if kind == "router":
                        pe.wait_ge(rw_split, 1)
                        wait_taken(pe, ("yT", b))
                        for t in range(QT):
                            tok = slice((QT * b + t) * P, (QT * b + t + 1) * P)
                            ins = three(misc[:, t * NE:(t + 1) * NE], yt_hi[:, tok], yt_lo[:, tok],
                                        rw_parts[:, 0, :], rw_parts[:, 1, :], True, True)
                        ins.then_inc(misc_made, 1)
                    if kind == "combT":
                        pe.wait_ge(route_pool, 4 * (b // 2) + 4)
                        for t in range(QT):
                            ins = nc.tensor.transpose(misc[0:NE, t * P:(t + 1) * P], comb[:, QT * (b % 2) + t, :], ident[:, :])
                        ins.then_inc(misc_made, 1)
                    if kind == "hidden" and b < NG * NSH:
                        g, j = divmod(b, NSH)
                        if b == 0:
                            pe.wait_ge(max_taken, 4 * NSTEP)
                            pe.wait_ge(w_split, PIECES)
                        elif b == 1:
                            pe.wait_ge(probs_made, 4 * NSTEP)
                        else:
                            pe.wait_ge(hid_made, b - 1)
                        wait_taken(pe, ("yT", 2 * g + 1))
                        for n, w in enumerate((W1, W3)):
                            c = slice(w + j * P, w + (j + 1) * P)
                            ins = three(shared_bank[b % 2][n][:, :], wf_hi[:, c], wf_lo[:, c], yt_hi[:, tokens(g)],
                                        yt_lo[:, tokens(g)], True, True)
                        ins.then_inc(up_made, 1)
                    if kind == "hidden" and b >= NG * NSH:
                        m = b - NG * NSH
                        g, e = divmod(m, NE)
                        if m in (1, 2):
                            pe.wait_ge(hid_made, NG * NSH)
                        if m >= 3:
                            pe.wait_ge(act_made, b - 2)
                        c = slice(E1 + e * P, E1 + (e + 1) * P)
                        three(expert_bank[m % 3][:, :], wf_hi[:, c], wf_lo[:, c], yt_hi[:, tokens(g)], yt_lo[:, tokens(g)],
                              True, True).then_inc(up_made, 1)
                    if kind == "down":
                        g, e = divmod(b, NE)
                        acc = max_bank[g % 2][:, :]
                        if e == 0:
                            pe.wait_ge(hid_made, NG * NSH - 1)
                            if g >= 2:
                                pe.wait_ge(acc_taken, g - 1)
                            for j in range(NSH):
                                pe.wait_ge(lo_made[j], g + 1)
                                c = slice(W2 + j * P, W2 + (j + 1) * P)
                                three(acc, wf_hi[:, c], wf_lo[:, c], sh_hi[:, j, tokens(g)], sh_lo[:, j, tokens(g)],
                                      j == 0, False)
                        n = NG * NSH + b
                        pe.wait_ge(lo_made[n % 2], n // 2 + 1)
                        c = slice(E2 + e * P, E2 + (e + 1) * P)
                        three(acc, wf_hi[:, c], wf_lo[:, c], hid_hi[:, b % 4, :], hid_lo[:, b % 4, :],
                              False, e == NE - 1).then_inc(down_made, 1)
                    if kind == "finT":
                        pe.wait_ge(acc_taken, b + 1)
                        if b:
                            pe.wait_ge(fin_stats, b)
                        for t in range(TPG):
                            ins = nc.tensor.transpose(pv_bank[:, t * P:(t + 1) * P], acc_t[:, t * P:(t + 1) * P], ident[:, :])
                        ins.then_inc(fin_made, 1)


_ARGS = ("x", "w_attn", "b_rows", "w_ffn")


def lay_out(i):
    def by_ab_d_pair(w):
        return w.reshape(-1, NAB, NPAIR, HD).transpose(0, 1, 3, 2).reshape(w.shape)

    wq, wk = (by_ab_d_pair(np.asarray(i[f"L0_attn_W{n}"])) for n in "qk")
    biases = [by_ab_d_pair(np.asarray(i[f"L0_attn_b{n}"])[None]).T for n in "qk"] + [np.asarray(i["L0_attn_bv"])[:, None]]
    w_attn = np.concatenate([wq, wk, np.asarray(i["L0_attn_Wv"]), np.asarray(i["L0_attn_Wo"])] + biases, axis=1)
    b_rows = np.concatenate([np.asarray(i["L0_attn_bo"]), np.asarray(i["L0_ffn_router_bias"])])[None]
    rows = lambda w: np.asarray(w).transpose(1, 0, 2).reshape(P, -1)
    w_ffn = np.concatenate([np.asarray(i["L0_ffn_sw1"]), np.asarray(i["L0_ffn_sw3"]), rows(i["L0_ffn_ew1"]),
                            rows(np.asarray(i["L0_ffn_sw2"]).reshape(NSH, P, P)), rows(i["L0_ffn_ew2"]),
                            np.asarray(i["L0_ffn_router_w"]).T], axis=1)
    return dict(zip(_ARGS, (np.asarray(i["L0_attn_x"]), w_attn, b_rows, w_ffn)))


def kernel(**inputs):
    import concourse.bacc as _bacc
    from concourse.bass_utils import run_bass_kernel_spmd as _run

    nc = _bacc.Bacc("TRN2", target_bir_lowering=False, num_devices=1)
    arrays = {f"{n}_dram": np.ascontiguousarray(a) for n, a in lay_out(inputs).items()}
    args = [nc.dram_tensor(n, a.shape, mybir.dt.from_np(a.dtype), kind="ExternalInput").ap() for n, a in arrays.items()]
    args.append(nc.dram_tensor("out_dram", (NB, S, P), F32, kind="ExternalOutput").ap())
    build_layer(nc, *args)
    return _run(nc, [arrays], core_ids=[0]).results[0]["out_dram"]
```
